# Optimizing a Trainium2 kernel written in Bass

```python
import numpy as np
import jax
import jax.numpy as jnp

def _softmax(x, axis=-1):
    return jax.nn.softmax(x, axis=axis)

def _gelu(x):
    return jax.nn.gelu(x, approximate=True)

def _silu(x):
    return jax.nn.silu(x)

def _sigmoid(x):
    return jax.nn.sigmoid(x)

def _layernorm(x, axis=-1, eps=1e-05):
    m = jnp.mean(x, axis=axis, keepdims=True)
    v = jnp.var(x, axis=axis, keepdims=True)
    return (x - m) / jnp.sqrt(v + eps)

def _scatter_add(tgt, idx, src, axis=0):
    return tgt.at[idx].add(src)

def _segment_sum(src, seg, n):
    return jax.ops.segment_sum(src, seg, n)
kernel_name = 'mk_decoder_postln_d2_seqx_r4_277614'

def setup_inputs(seed: int=0):
    np.random.seed(seed)
    _w = jnp.asarray

    def _rec_inputs():
        import jax
        import jax.numpy as jnp
        _rk = jax.random.key(seed)
        x = -0.0002928 + 1 * jax.random.normal(jax.random.fold_in(_rk, 1), (2, 1024, 256), jnp.float32)
        _lenS = 1024 - jax.random.randint(jax.random.fold_in(_rk, 7), (2,), 0, max(1, 1024 // 4) + 1, jnp.int32)
        _lenS2 = 64 - jax.random.randint(jax.random.fold_in(_rk, 8), (2,), 0, max(1, 64 // 4) + 1, jnp.int32)
        _ctx_1024P = jax.random.normal(jax.random.fold_in(_rk, 11), (2, 16, 256), jnp.float32)
        _ctx_1024c = jax.random.dirichlet(jax.random.fold_in(_rk, 511), 0.3 * jnp.ones((16,), jnp.float32), (2, 64))
        _ctx_1024t = jnp.einsum('bsk,bkd->bsd', _ctx_1024c, _ctx_1024P)
        _ctx_1024t = _ctx_1024t * jax.lax.rsqrt(jnp.mean(jnp.square(_ctx_1024t)) + 1e-12) * 0.953939
        ctx_1024 = -1.39393e-06 + 0.999914 * (_ctx_1024t + 0.3 * jax.random.normal(jax.random.fold_in(_rk, 611), (2, 64, 256), jnp.float32))
        _validS = jnp.arange(1024)[None, :] < _lenS[:, None]
        _validS2 = jnp.arange(64)[None, :] < _lenS2[:, None]
        _causal = jnp.tril(jnp.ones((1024, 1024), dtype=bool))
        mask_BxS2_if1 = jnp.where(jnp.ones((2, 64), dtype=bool), 1, 0).astype(jnp.int32)
        mask_BxS2_ik1 = jnp.where(jnp.broadcast_to(_validS2[:, :], (2, 64)), 1, 0).astype(jnp.int32)
        return (x, ctx_1024, mask_BxS2_if1, mask_BxS2_ik1)
    x, ctx_1024, mask_BxS2_if1, mask_BxS2_ik1 = _rec_inputs()

    def _L0_attn_setup():
        import jax, jax.numpy as jnp
        import numpy as np
        B, S, D = (2, 512, 256)
        NH, KVH = (16, 4)
        HD = D // NH
        ROPE_BASE = 10000.0

        def rotate_half(x):
            half = x.shape[-1] // 2
            x1, x2 = (x[..., :half], x[..., half:])
            return jnp.concatenate((-x2, x1), axis=-1)

        def rope_cache(seq_len, head_dim, base, dtype):
            half = head_dim // 2
            inv_freq = 1.0 / base ** (jnp.arange(half, dtype=jnp.float32) / max(1, half))
            t = jnp.arange(seq_len, dtype=jnp.float32)
            freqs = jnp.einsum('i,j->ij', t, inv_freq)
            emb = jnp.concatenate((freqs, freqs), axis=-1)
            cos = jnp.cos(emb)[None, None].astype(dtype)
            sin = jnp.sin(emb)[None, None].astype(dtype)
            return (sin, cos)
        key = jax.random.key(seed)
        ks = jax.random.split(key, 5)
        s = 0.02
        return {'x': jax.random.normal(ks[0], (B, S, D), dtype=jnp.float32), 'Wq': jax.random.normal(ks[1], (D, D), dtype=jnp.float32) * s, 'Wk': jax.random.normal(ks[2], (D, KVH * HD), dtype=jnp.float32) * s, 'Wv': jax.random.normal(ks[3], (D, KVH * HD), dtype=jnp.float32) * s, 'Wo': jax.random.normal(ks[4], (D, D), dtype=jnp.float32) * s}
    _L0_attn_all = _L0_attn_setup()
    _L0_attn_in = {k: v for k, v in _L0_attn_all.items() if k in ('Wq', 'Wk', 'Wv', 'Wo')}
    del _L0_attn_all

    def _L0_xattn_setup():
        import jax, jax.numpy as jnp
        import numpy as np
        D_MODEL = 256
        N_HEADS = 16
        D_K = D_MODEL // N_HEADS
        B, L = (2, 512)

        def _dense_bf16(x, W, b):
            return jnp.matmul(x.astype(jnp.bfloat16), W.astype(jnp.bfloat16)) + b.astype(jnp.bfloat16)

        def _attention(q, k, v, mask):
            Lq, Ls, dk = (q.shape[2], k.shape[2], q.shape[3])
            scale = 1.0 / np.sqrt(dk)
            scores = jnp.einsum('bhqd,bhkd->bhqk', q, k) * scale
            causal = jnp.tril(jnp.ones((Lq, Ls), bool))
            full_mask = causal[None, None] & (mask[:, None, None, :] > 0)
            scores = jnp.where(full_mask, scores, -jnp.inf)
            p = jax.nn.softmax(scores, axis=-1)
            return jnp.einsum('bhqk,bhkd->bhqd', p, v)
        key = jax.random.key(seed)
        ks = jax.random.split(key, 8)
        inp = {'q': jax.random.normal(ks[0], (B, L, D_MODEL), jnp.float32), 'k': jax.random.normal(ks[1], (B, L, D_MODEL), jnp.float32), 'v': jax.random.normal(ks[2], (B, L, D_MODEL), jnp.float32), 'mask': jnp.ones((B, L), jnp.int32), 'Wq': jax.random.normal(ks[3], (D_MODEL, D_MODEL), jnp.float32) * 0.02, 'bq': jnp.zeros((D_MODEL,), jnp.float32), 'Wk': jax.random.normal(ks[4], (D_MODEL, D_MODEL), jnp.float32) * 0.02, 'bk': jnp.zeros((D_MODEL,), jnp.float32), 'Wv': jax.random.normal(ks[5], (D_MODEL, D_MODEL), jnp.float32) * 0.02, 'bv': jnp.zeros((D_MODEL,), jnp.float32), 'Wo': jax.random.normal(ks[6], (D_MODEL, D_MODEL), jnp.float32) * 0.02, 'bo': jnp.zeros((D_MODEL,), jnp.float32)}
        return inp
    _L0_xattn_all = _L0_xattn_setup()
    _L0_xattn_in = {k: v for k, v in _L0_xattn_all.items() if k in ('Wq', 'bq', 'Wk', 'bk', 'Wv', 'bv', 'Wo', 'bo')}
    del _L0_xattn_all

    def _L0_ffn_setup():
        import jax, jax.numpy as jnp
        import numpy as np
        H = 256
        I = 4 * H
        E = 8
        K = 2
        B, S = (2, 256)
        STD = 0.02 / np.sqrt(H)
        key = jax.random.key(seed)
        ks = jax.random.split(key, 8)
        x = jax.random.normal(ks[0], (B, S, H), dtype=jnp.float32)
        gate_w = jax.random.normal(ks[1], (H, E), dtype=jnp.float32) * STD
        bias = jnp.zeros((E,), dtype=jnp.float32)
        up_w = jax.random.normal(ks[2], (E, H, I), dtype=jnp.float32) * STD
        up_b = jnp.zeros((E, I), dtype=jnp.float32)
        down_w = jax.random.normal(ks[3], (E, I, H), dtype=jnp.float32) * STD
        down_b = jnp.zeros((E, H), dtype=jnp.float32)
        sw_up = jax.random.normal(ks[4], (H, I), dtype=jnp.float32) * STD
        sb_up = jnp.zeros((I,), dtype=jnp.float32)
        sw_down = jax.random.normal(ks[5], (I, H), dtype=jnp.float32) * STD
        sb_down = jnp.zeros((H,), dtype=jnp.float32)
        return {'x': x, 'gate_w': gate_w, 'bias': bias, 'up_w': up_w, 'up_b': up_b, 'down_w': down_w, 'down_b': down_b, 'sw_up': sw_up, 'sb_up': sb_up, 'sw_down': sw_down, 'sb_down': sb_down}
    _L0_ffn_all = _L0_ffn_setup()
    _L0_ffn_in = {k: v for k, v in _L0_ffn_all.items() if k in ('gate_w', 'bias', 'up_w', 'up_b', 'down_w', 'down_b', 'sw_up', 'sb_up', 'sw_down', 'sb_down')}
    del _L0_ffn_all

    def _L1_attn_setup():
        import jax, jax.numpy as jnp
        import numpy as np
        from jax import lax
        LN_EPS = 1e-05
        B, T, C = (4, 1024, 256)

        def _layernorm(x, w, b):
            mu = jnp.mean(x, axis=-1, keepdims=True)
            var = jnp.mean((x - mu) ** 2, axis=-1, keepdims=True)
            return (x - mu) * lax.rsqrt(var + LN_EPS) * w + b
        key = jax.random.key(seed)
        ks = jax.random.split(key, 12)
        s = 1.0 / np.sqrt(C)
        return {'x': jax.random.normal(ks[0], (B, T, C), dtype=jnp.float32), 'time_mix_k': jax.random.uniform(ks[1], (C,), dtype=jnp.float32), 'time_mix_v': jax.random.uniform(ks[2], (C,), dtype=jnp.float32), 'time_mix_r': jax.random.uniform(ks[3], (C,), dtype=jnp.float32), 'time_decay': jnp.zeros((C,), dtype=jnp.float32), 'time_first': jnp.zeros((C,), dtype=jnp.float32), 'Wk': jax.random.uniform(ks[4], (C, C), jnp.float32, -s, s), 'Wv': jax.random.uniform(ks[5], (C, C), jnp.float32, -s, s), 'Wr': jax.random.uniform(ks[6], (C, C), jnp.float32, -s, s), 'Wo': jax.random.uniform(ks[7], (C, C), jnp.float32, -s, s), 'ln_w': jnp.ones((C,), dtype=jnp.float32), 'ln_b': jnp.zeros((C,), dtype=jnp.float32)}
    _L1_attn_all = _L1_attn_setup()
    _L1_attn_in = {k: v for k, v in _L1_attn_all.items() if k in ('time_mix_k', 'time_mix_v', 'time_mix_r', 'time_decay', 'time_first', 'Wk', 'Wv', 'Wr', 'Wo', 'ln_w', 'ln_b')}
    del _L1_attn_all

    def _L1_xattn_setup():
        import jax, jax.numpy as jnp
        import numpy as np
        D = 256
        B, LQ, LK = (8, 512, 512)
        NEG = -1000000000.0
        key = jax.random.key(seed)
        ks = jax.random.split(key, 8)
        query = jax.random.normal(ks[0], (B, LQ, D), dtype=jnp.float32)
        k_in = jax.random.normal(ks[1], (B, LK, D), dtype=jnp.float32)
        value = jax.random.normal(ks[2], (B, LK, D), dtype=jnp.float32)
        mask = jax.random.randint(ks[3], (B, LK), 0, 2, dtype=jnp.int32)
        s = 1.0 / np.sqrt(D)
        Wq_w = jax.random.normal(ks[4], (D, D), dtype=jnp.float32) * s
        Wq_b = jnp.zeros((D,), dtype=jnp.float32)
        Wk_w = jax.random.normal(ks[5], (D, D), dtype=jnp.float32) * s
        Wk_b = jnp.zeros((D,), dtype=jnp.float32)
        return {'query': query, 'key': k_in, 'value': value, 'mask': mask, 'Wq_w': Wq_w, 'Wq_b': Wq_b, 'Wk_w': Wk_w, 'Wk_b': Wk_b}
    _L1_xattn_all = _L1_xattn_setup()
    _L1_xattn_in = {k: v for k, v in _L1_xattn_all.items() if k in ('Wq_w', 'Wq_b', 'Wk_w', 'Wk_b')}
    del _L1_xattn_all

    def _L1_ffn_setup():
        import jax, jax.numpy as jnp
        import numpy as np
        B, S, H = (2, 256, 256)
        E, F = (16, 128)
        G, TOPK_G, TOPK = (4, 2, 4)
        N_SHARED = 2
        ROUTE_SCALE = 1.0
        FS = N_SHARED * F

        def _gate(x, w_gate):
            T = x.shape[0]
            scores = jax.nn.sigmoid(x @ w_gate.T)
            sv = scores.reshape(T, G, E // G)
            group_scores = jax.lax.top_k(sv, 2)[0].sum(-1)
            top_groups = jax.lax.top_k(group_scores, TOPK_G)[1]
            allowed = jnp.zeros((T, G), dtype=bool).at[jnp.arange(T)[:, None], top_groups].set(True)
            masked = jnp.where(allowed[:, :, None], sv, -jnp.inf).reshape(T, E)
            _, idx = jax.lax.top_k(masked, TOPK)
            w = jnp.take_along_axis(scores, idx, axis=1)
            w = w / (w.sum(-1, keepdims=True) + 1e-06) * ROUTE_SCALE
            return (w, idx)

        def _swiglu(x, w1, w3, w2):
            return jax.nn.silu(x @ w1.T) * (x @ w3.T) @ w2.T
        key = jax.random.key(seed)
        ks = jax.random.split(key, 8)
        scale = 0.02
        return {'hidden_states': jax.random.normal(ks[0], (B, S, H), dtype=jnp.float32), 'w_gate': jax.random.normal(ks[1], (E, H), dtype=jnp.float32) * scale, 'w1_e': jax.random.normal(ks[2], (E, F, H), dtype=jnp.float32) * scale, 'w3_e': jax.random.normal(ks[3], (E, F, H), dtype=jnp.float32) * scale, 'w2_e': jax.random.normal(ks[4], (E, H, F), dtype=jnp.float32) * scale, 'w1_s': jax.random.normal(ks[5], (FS, H), dtype=jnp.float32) * scale, 'w3_s': jax.random.normal(ks[6], (FS, H), dtype=jnp.float32) * scale, 'w2_s': jax.random.normal(ks[7], (H, FS), dtype=jnp.float32) * scale}
    _L1_ffn_all = _L1_ffn_setup()
    _L1_ffn_in = {k: v for k, v in _L1_ffn_all.items() if k in ('w_gate', 'w1_e', 'w3_e', 'w2_e', 'w1_s', 'w3_s', 'w2_s')}
    del _L1_ffn_all
    return {'x': x, 'ctx_1024': ctx_1024, 'mask_BxS2_if1': mask_BxS2_if1, 'mask_BxS2_ik1': mask_BxS2_ik1, 'L0_attn_Wq': _L0_attn_in['Wq'], 'L0_attn_Wk': _L0_attn_in['Wk'], 'L0_attn_Wv': _L0_attn_in['Wv'], 'L0_attn_Wo': _L0_attn_in['Wo'], 'L0_xattn_Wq': _L0_xattn_in['Wq'], 'L0_xattn_bq': _L0_xattn_in['bq'], 'L0_xattn_Wk': _L0_xattn_in['Wk'], 'L0_xattn_bk': _L0_xattn_in['bk'], 'L0_xattn_Wv': _L0_xattn_in['Wv'], 'L0_xattn_bv': _L0_xattn_in['bv'], 'L0_xattn_Wo': _L0_xattn_in['Wo'], 'L0_xattn_bo': _L0_xattn_in['bo'], 'L0_ffn_gate_w': _L0_ffn_in['gate_w'], 'L0_ffn_bias': _L0_ffn_in['bias'], 'L0_ffn_up_w': _L0_ffn_in['up_w'], 'L0_ffn_up_b': _L0_ffn_in['up_b'], 'L0_ffn_down_w': _L0_ffn_in['down_w'], 'L0_ffn_down_b': _L0_ffn_in['down_b'], 'L0_ffn_sw_up': _L0_ffn_in['sw_up'], 'L0_ffn_sb_up': _L0_ffn_in['sb_up'], 'L0_ffn_sw_down': _L0_ffn_in['sw_down'], 'L0_ffn_sb_down': _L0_ffn_in['sb_down'], 'L1_attn_time_mix_k': _L1_attn_in['time_mix_k'], 'L1_attn_time_mix_v': _L1_attn_in['time_mix_v'], 'L1_attn_time_mix_r': _L1_attn_in['time_mix_r'], 'L1_attn_time_decay': _L1_attn_in['time_decay'], 'L1_attn_time_first': _L1_attn_in['time_first'], 'L1_attn_Wk': _L1_attn_in['Wk'], 'L1_attn_Wv': _L1_attn_in['Wv'], 'L1_attn_Wr': _L1_attn_in['Wr'], 'L1_attn_Wo': _L1_attn_in['Wo'], 'L1_attn_ln_w': _L1_attn_in['ln_w'], 'L1_attn_ln_b': _L1_attn_in['ln_b'], 'L1_xattn_Wq_w': _L1_xattn_in['Wq_w'], 'L1_xattn_Wq_b': _L1_xattn_in['Wq_b'], 'L1_xattn_Wk_w': _L1_xattn_in['Wk_w'], 'L1_xattn_Wk_b': _L1_xattn_in['Wk_b'], 'L1_ffn_w_gate': _L1_ffn_in['w_gate'], 'L1_ffn_w1_e': _L1_ffn_in['w1_e'], 'L1_ffn_w3_e': _L1_ffn_in['w3_e'], 'L1_ffn_w2_e': _L1_ffn_in['w2_e'], 'L1_ffn_w1_s': _L1_ffn_in['w1_s'], 'L1_ffn_w3_s': _L1_ffn_in['w3_s'], 'L1_ffn_w2_s': _L1_ffn_in['w2_s']}

def reference(x, ctx_1024, mask_BxS2_if1, mask_BxS2_ik1, L0_attn_Wq, L0_attn_Wk, L0_attn_Wv, L0_attn_Wo, L0_xattn_Wq, L0_xattn_bq, L0_xattn_Wk, L0_xattn_bk, L0_xattn_Wv, L0_xattn_bv, L0_xattn_Wo, L0_xattn_bo, L0_ffn_gate_w, L0_ffn_bias, L0_ffn_up_w, L0_ffn_up_b, L0_ffn_down_w, L0_ffn_down_b, L0_ffn_sw_up, L0_ffn_sb_up, L0_ffn_sw_down, L0_ffn_sb_down, L1_attn_time_mix_k, L1_attn_time_mix_v, L1_attn_time_mix_r, L1_attn_time_decay, L1_attn_time_first, L1_attn_Wk, L1_attn_Wv, L1_attn_Wr, L1_attn_Wo, L1_attn_ln_w, L1_attn_ln_b, L1_xattn_Wq_w, L1_xattn_Wq_b, L1_xattn_Wk_w, L1_xattn_Wk_b, L1_ffn_w_gate, L1_ffn_w1_e, L1_ffn_w3_e, L1_ffn_w2_e, L1_ffn_w1_s, L1_ffn_w3_s, L1_ffn_w2_s):
    import jax
    import jax.numpy as jnp

    def _L0_attn_ref(x, Wq, Wk, Wv, Wo):
        import jax, jax.numpy as jnp
        import numpy as np
        B, S, D = (2, 512, 256)
        NH, KVH = (16, 4)
        HD = D // NH
        ROPE_BASE = 10000.0

        def rotate_half(x):
            half = x.shape[-1] // 2
            x1, x2 = (x[..., :half], x[..., half:])
            return jnp.concatenate((-x2, x1), axis=-1)

        def rope_cache(seq_len, head_dim, base, dtype):
            half = head_dim // 2
            inv_freq = 1.0 / base ** (jnp.arange(half, dtype=jnp.float32) / max(1, half))
            t = jnp.arange(seq_len, dtype=jnp.float32)
            freqs = jnp.einsum('i,j->ij', t, inv_freq)
            emb = jnp.concatenate((freqs, freqs), axis=-1)
            cos = jnp.cos(emb)[None, None].astype(dtype)
            sin = jnp.sin(emb)[None, None].astype(dtype)
            return (sin, cos)
        bsz, seq_len, _ = x.shape
        scale = HD ** (-0.5)
        q = (x @ Wq).reshape(bsz, seq_len, NH, HD).transpose(0, 2, 1, 3)
        k = (x @ Wk).reshape(bsz, seq_len, KVH, HD).transpose(0, 2, 1, 3)
        v = (x @ Wv).reshape(bsz, seq_len, KVH, HD).transpose(0, 2, 1, 3)
        sin, cos = rope_cache(seq_len, HD, ROPE_BASE, q.dtype)
        q = q * cos + rotate_half(q) * sin
        k = k * cos + rotate_half(k) * sin
        rep = NH // KVH
        k = jnp.repeat(k, rep, axis=1)
        v = jnp.repeat(v, rep, axis=1)
        att = jnp.einsum('bhqd,bhkd->bhqk', q, k) * scale
        causal = jnp.tril(jnp.ones((seq_len, seq_len), dtype=bool))
        att = jnp.where(causal, att, jnp.finfo(att.dtype).min)
        att = jax.nn.softmax(att, axis=-1)
        y = jnp.einsum('bhqk,bhkd->bhqd', att, v)
        y = y.transpose(0, 2, 1, 3).reshape(bsz, seq_len, NH * HD)
        return y @ Wo

    def _L0_xattn_ref(q, k, v, mask, Wq, bq, Wk, bk, Wv, bv, Wo, bo):
        import jax, jax.numpy as jnp
        import numpy as np
        D_MODEL = 256
        N_HEADS = 16
        D_K = D_MODEL // N_HEADS
        B, L = (2, 512)

        def _dense_bf16(x, W, b):
            return jnp.matmul(x.astype(jnp.bfloat16), W.astype(jnp.bfloat16)) + b.astype(jnp.bfloat16)

        def _attention(q, k, v, mask):
            Lq, Ls, dk = (q.shape[2], k.shape[2], q.shape[3])
            scale = 1.0 / np.sqrt(dk)
            scores = jnp.einsum('bhqd,bhkd->bhqk', q, k) * scale
            causal = jnp.tril(jnp.ones((Lq, Ls), bool))
            full_mask = causal[None, None] & (mask[:, None, None, :] > 0)
            scores = jnp.where(full_mask, scores, -jnp.inf)
            p = jax.nn.softmax(scores, axis=-1)
            return jnp.einsum('bhqk,bhkd->bhqd', p, v)
        query = _dense_bf16(q, Wq, bq).astype(jnp.float32)
        key_p = _dense_bf16(k, Wk, bk).astype(jnp.float32)
        val_p = _dense_bf16(v, Wv, bv).astype(jnp.float32)
        Bb, Lt, _ = query.shape
        Ls = key_p.shape[1]
        query = query.reshape(Bb, Lt, N_HEADS, D_K).transpose(0, 2, 1, 3)
        key_p = key_p.reshape(Bb, Ls, N_HEADS, D_K).transpose(0, 2, 1, 3)
        val_p = val_p.reshape(Bb, Ls, N_HEADS, D_K).transpose(0, 2, 1, 3)
        x = _attention(query, key_p, val_p, mask)
        x = x.transpose(0, 2, 1, 3).reshape(Bb, Lt, D_MODEL)
        out = _dense_bf16(x, Wo, bo)
        return out.astype(jnp.float32)

    def _L0_ffn_ref(x, gate_w, bias, up_w, up_b, down_w, down_b, sw_up, sb_up, sw_down, sb_down):
        import jax, jax.numpy as jnp
        import numpy as np
        H = 256
        I = 4 * H
        E = 8
        K = 2
        B, S = (2, 256)
        STD = 0.02 / np.sqrt(H)
        b, s, h = x.shape
        xf = x.reshape(-1, h)
        T = xf.shape[0]
        scores = jax.nn.sigmoid(xf @ gate_w + bias)
        top_scores, top_idx = jax.lax.top_k(scores, K)
        top_scores = top_scores / (jnp.sum(top_scores, axis=-1, keepdims=True) + 1e-06)
        w = jnp.zeros((T, E), dtype=xf.dtype).at[jnp.arange(T)[:, None], top_idx].add(top_scores)
        up = jnp.einsum('th,ehi->tei', xf, up_w) + up_b
        hact = jax.nn.gelu(up, approximate=False)
        eo = jnp.einsum('tei,eih->teh', hact, down_w) + down_b
        combined = jnp.einsum('teh,te->th', eo * 0.1, w)
        shared = (jax.nn.gelu(xf @ sw_up + sb_up, approximate=False) @ sw_down + sb_down) * 0.1
        out = (shared + combined).reshape(b, s, h)
        out = out / (jnp.max(jnp.abs(out), axis=-1, keepdims=True) + 1e-06)
        return out

    def _L1_attn_ref(x, time_mix_k, time_mix_v, time_mix_r, time_decay, time_first, Wk, Wv, Wr, Wo, ln_w, ln_b):
        import jax, jax.numpy as jnp
        import numpy as np
        from jax import lax
        LN_EPS = 1e-05
        B, T, C = (4, 1024, 256)

        def _layernorm(x, w, b):
            mu = jnp.mean(x, axis=-1, keepdims=True)
            var = jnp.mean((x - mu) ** 2, axis=-1, keepdims=True)
            return (x - mu) * lax.rsqrt(var + LN_EPS) * w + b
        xt = _layernorm(x, ln_w, ln_b)
        x_prev = jnp.pad(xt[:, :-1], ((0, 0), (1, 0), (0, 0)))
        decay = jax.nn.sigmoid(time_decay)
        first = jnp.exp(time_first)
        mk, mv, mr = (time_mix_k, time_mix_v, time_mix_r)
        K = jnp.einsum('btc,dc->btd', xt * mk + x_prev * (1.0 - mk), Wk)
        V = jnp.einsum('btc,dc->btd', xt * mv + x_prev * (1.0 - mv), Wv)
        R = jax.nn.sigmoid(jnp.einsum('btc,dc->btd', xt * mr + x_prev * (1.0 - mr), Wr))

        def step(state, k_t):
            state = state * decay + k_t
            return (state, state)
        _, S = lax.scan(step, jnp.zeros((x.shape[0], K.shape[-1]), x.dtype), jnp.swapaxes(K, 0, 1))
        S = jnp.swapaxes(S, 0, 1)
        rwkv = (S * first + K) * V
        y = jnp.einsum('btc,dc->btd', R * rwkv, Wo)
        return x + y

    def _L1_xattn_ref(query, key, value, mask, Wq_w, Wq_b, Wk_w, Wk_b):
        import jax, jax.numpy as jnp
        import numpy as np
        D = 256
        B, LQ, LK = (8, 512, 512)
        NEG = -1000000000.0
        q = jnp.einsum('bld,ed->ble', query, Wq_w) + Wq_b
        k = jnp.einsum('bld,ed->ble', key, Wk_w) + Wk_b
        scale = 1.0 / jnp.sqrt(jnp.asarray(D, dtype=q.dtype))
        aw = jnp.einsum('bqd,bkd->bqk', q, k) * scale
        m = mask.astype(aw.dtype)[:, None, :]
        aw = aw * m
        aw = jnp.where(m == 0, jnp.asarray(NEG, dtype=aw.dtype), aw)
        attn = jax.nn.softmax(aw, axis=-1)
        return jnp.einsum('bqk,bkd->bqd', attn, value)

    def _L1_ffn_ref(hidden_states, w_gate, w1_e, w3_e, w2_e, w1_s, w3_s, w2_s):
        import jax, jax.numpy as jnp
        import numpy as np
        B, S, H = (2, 256, 256)
        E, F = (16, 128)
        G, TOPK_G, TOPK = (4, 2, 4)
        N_SHARED = 2
        ROUTE_SCALE = 1.0
        FS = N_SHARED * F

        def _gate(x, w_gate):
            T = x.shape[0]
            scores = jax.nn.sigmoid(x @ w_gate.T)
            sv = scores.reshape(T, G, E // G)
            group_scores = jax.lax.top_k(sv, 2)[0].sum(-1)
            top_groups = jax.lax.top_k(group_scores, TOPK_G)[1]
            allowed = jnp.zeros((T, G), dtype=bool).at[jnp.arange(T)[:, None], top_groups].set(True)
            masked = jnp.where(allowed[:, :, None], sv, -jnp.inf).reshape(T, E)
            _, idx = jax.lax.top_k(masked, TOPK)
            w = jnp.take_along_axis(scores, idx, axis=1)
            w = w / (w.sum(-1, keepdims=True) + 1e-06) * ROUTE_SCALE
            return (w, idx)

        def _swiglu(x, w1, w3, w2):
            return jax.nn.silu(x @ w1.T) * (x @ w3.T) @ w2.T
        shape = hidden_states.shape
        x = hidden_states.reshape(-1, H)
        weights, idx = _gate(x, w_gate)
        combine = (jax.nn.one_hot(idx, E, dtype=x.dtype) * weights[..., None]).sum(1)
        g = jax.nn.silu(jnp.einsum('th,efh->tef', x, w1_e))
        u = jnp.einsum('th,efh->tef', x, w3_e)
        routed = jnp.einsum('tef,ehf,te->th', g * u, w2_e, combine)
        shared = _swiglu(x, w1_s, w3_s, w2_s)
        return (routed + shared).reshape(shape)
    x = _layernorm(x + _L0_attn_ref(x, L0_attn_Wq, L0_attn_Wk, L0_attn_Wv, L0_attn_Wo), axis=-1)
    x = _layernorm(x + _L0_xattn_ref(x, ctx_1024, ctx_1024, mask_BxS2_if1, L0_xattn_Wq, L0_xattn_bq, L0_xattn_Wk, L0_xattn_bk, L0_xattn_Wv, L0_xattn_bv, L0_xattn_Wo, L0_xattn_bo), axis=-1)
    x = _layernorm(x + _L0_ffn_ref(x, L0_ffn_gate_w, L0_ffn_bias, L0_ffn_up_w, L0_ffn_up_b, L0_ffn_down_w, L0_ffn_down_b, L0_ffn_sw_up, L0_ffn_sb_up, L0_ffn_sw_down, L0_ffn_sb_down), axis=-1)
    x = _layernorm(x + _L1_attn_ref(x, L1_attn_time_mix_k, L1_attn_time_mix_v, L1_attn_time_mix_r, L1_attn_time_decay, L1_attn_time_first, L1_attn_Wk, L1_attn_Wv, L1_attn_Wr, L1_attn_Wo, L1_attn_ln_w, L1_attn_ln_b), axis=-1)
    x = _layernorm(x + _L1_xattn_ref(x, ctx_1024, ctx_1024, mask_BxS2_ik1, L1_xattn_Wq_w, L1_xattn_Wq_b, L1_xattn_Wk_w, L1_xattn_Wk_b), axis=-1)
    x = _layernorm(x + _L1_ffn_ref(x, L1_ffn_w_gate, L1_ffn_w1_e, L1_ffn_w3_e, L1_ffn_w2_e, L1_ffn_w1_s, L1_ffn_w3_s, L1_ffn_w2_s), axis=-1)
    return x

_drawn_inputs = setup_inputs


def setup_inputs(seed=0):
    import zlib

    import numpy as np

    out = dict(_drawn_inputs(seed))
    spreads = {'L0_xattn_bq': (0.0, 0.8),
     'L0_xattn_bk': (0.0, 0.8),
     'L0_xattn_bv': (0.0, 0.27),
     'L0_xattn_bo': (0.0, 0.1),
     'L0_ffn_bias': (0.0, 0.1),
     'L0_ffn_up_b': (0.0, 0.8),
     'L0_ffn_down_b': (0.0, 0.1),
     'L0_ffn_sb_up': (0.0, 0.8),
     'L0_ffn_sb_down': (0.0, 0.1),
     'L1_attn_time_decay': (0.0, 0.8),
     'L1_attn_time_first': (0.0, 0.8),
     'L1_attn_ln_w': (1.0, 0.6),
     'L1_attn_ln_b': (0.0, 0.561),
     'L1_xattn_Wq_b': (0.0, 0.404),
     'L1_xattn_Wk_b': (0.0, 0.8)}
    factors = {'L0_attn_Wq': 8.0,
     'L0_attn_Wk': 8.0,
     'L0_attn_Wv': 5.761,
     'L0_attn_Wo': 6.461,
     'L0_xattn_Wq': 8.0,
     'L0_xattn_Wk': 8.0,
     'L0_ffn_up_w': 8.0,
     'L0_ffn_down_w': 8.0,
     'L0_ffn_sw_up': 8.0,
     'L0_ffn_sw_down': 8.0,
     'L1_attn_time_mix_r': 6.998,
     'L1_attn_Wr': 3.069,
     'L1_ffn_w_gate': 8.0,
     'L1_ffn_w1_e': 8.0,
     'L1_ffn_w3_e': 8.0,
     'L1_ffn_w2_e': 8.0,
     'L1_ffn_w1_s': 3.362,
     'L1_ffn_w3_s': 3.405,
     'L1_ffn_w2_s': 3.325}
    for name, (base, spread) in spreads.items():
        noise = np.random.default_rng([zlib.crc32(name.encode()), seed]).standard_normal(out[name].shape)
        drawn = base * np.exp(spread * noise) if base else spread * noise
        out[name] = jnp.asarray(drawn.astype(out[name].dtype))
    for name, factor in factors.items():
        out[name] = (out[name] * factor).astype(out[name].dtype)
    return out
```

```python
from contextlib import ExitStack

import numpy as np

import concourse.bass as bass
from concourse import mybir

F32 = mybir.dt.float32
BF16 = mybir.dt.bfloat16
I32 = mybir.dt.int32
ALU = mybir.AluOpType
ACT = mybir.ActivationFunctionType
AX_X = mybir.AxisListType.X
ds = bass.ds

P = 128
B, S, D = 2, 1024, 256
T = B * S
NT = T // P
TB = S // P
KD = D // P
NH, KVH, HD = 16, 4, 16
REP = NH // KVH
LN_EPS = 1e-5
NEG = -1e30
LOWEST = -3e38


def bcast(ap, dim, n):
    shape = list(ap.shape)
    shape.insert(dim, n)
    return ap.unsqueeze(dim).to_broadcast(shape)


class Scope:

    def __init__(self, nc, name):
        self.nc, self.name, self.stack, self.sems = nc, name, ExitStack(), []

    def sb(self, name, shape, dt=F32):
        return self.stack.enter_context(self.nc.sbuf_tensor(f"{self.name}_{name}", shape, dt))

    def ps(self, name, shape, dt=F32):
        return self.stack.enter_context(self.nc.psum_tensor(f"{self.name}_{name}", shape, dt))

    def sem(self, name):
        s = self.stack.enter_context(self.nc.semaphore(f"{self.name}_{name}"))
        self.sems.append(s.num)
        return s

    def close(self, spent=None):
        self.stack.close()
        if spent is not None:
            spent += self.sems


def zero_semaphores(nc, spent):
    nums, runs = sorted(spent), []
    for n in nums:
        if runs and runs[-1][1] == n:
            runs[-1][1] = n + 1
        else:
            runs.append([n, n + 1])
    with nc.Block() as block:

        @block.gpsimd
        def _(pool):
            for lo, hi in runs:
                pool.sem_clear(range(lo, hi))
    spent.clear()


def settle(eng, passed):
    eng.sem_inc(passed, 1)


class Chain:

    def __init__(self, eng, sem, passed=None):
        self.eng, self.sem, self.n, self.base, self.passed = eng, sem, 0, 0, passed

    def done(self, ins):
        ins.then_inc(self.sem, 1)
        self.n += 1
        return self.n

    def wait(self, n=None):
        self.eng.wait_ge(self.sem, self.base + (self.n if n is None else n))
        if self.passed is not None and not isinstance(self.base, int):
            settle(self.eng, self.passed)

    def link(self, ins):
        self.done(ins)
        self.wait()

    def enter(self, i, per):
        self.before, self.per = self.n, per
        self.base, self.n = self.n + i * per, 0

    def leave(self, trips):
        assert self.n == self.per, (self.n, self.per)
        self.base, self.n = 0, self.before + self.per * trips


PARTS = 6
MROW = PARTS * HD


def attention_plan():
    units = [(c, kt, pr) for c in range(2) for kt in range(4 * c + 4) for pr in range(2)]
    maxes = [(r, t, c) for r in range(REP) for t in range(TB) for c in range(t // 4 + 1)]
    return units, maxes


UNITS, MAXES = attention_plan()
NU, NM = len(UNITS), len(MAXES)


def iteration_plan():
    plan = []
    emitted, nxt, places = 0, 1, 4 * (NU // 2 - 2)

    def maxima(place):
        nonlocal emitted, nxt
        while emitted < min(NM, -(-(place + 1) * NM // places)):
            if nxt < REP and emitted >= 12 * nxt - 3:
                plan.append(("trQ", nxt))
                nxt += 1
            plan.append(("mx", emitted))
            emitted += 1

    for m in range(NU // 2):
        plan.append(("st", 2 * m))
        maxima(4 * m)
        plan.append(("st", 2 * m + 1))
        maxima(4 * m + 1)
        if m:
            plan += [("pv", 2 * m - 2), ("pv", 2 * m - 1)]
        if m == 5:
            plan.append(("otr", 0))
        maxima(4 * m + 2)
        maxima(4 * m + 3)
        if m >= NU // 2 - 2:
            plan += [("trm", 2 * m - NU + 4), ("trm", 2 * m - NU + 5)]
    plan += [("trK", 0), ("pv", NU - 2), ("pv", NU - 1), ("trQ", 0), ("otr", 1)]
    assert emitted == NM and nxt == REP
    return plan


PLAN = iteration_plan()
PROLOGUE = ([("trK", -1)] + [x for r in range(REP) for x in [("trQ", r - REP if r == 0 else r)] + [("mx", 12 * r + k) for k in range(12)]]
            + [("trm", r) for r in range(REP)] + [("trK", 0), ("trQ", 0)])
PLAN_6 = [x for x in PLAN if x not in (("trK", 0), ("trQ", 0))]
PLAN_7 = [x for x in PLAN if x[0] in ("st", "pv", "otr")]
TRANSPOSES = ("trm", "trK", "trQ", "otr")
RING = 3


class Placed:

    def __init__(self, plan, base, uses=TRANSPOSES + ("mx",)):
        self.plan, self.base, self.at, self.count = plan, base, [], [0] * len(base)
        turn = 0
        for step in plan:
            bank = None
            if step[0] in uses:
                bank = turn % len(base)
                turn += 1
                self.count[bank] += 1
            self.at.append((bank, self.count[bank] if bank is not None else None))

    def steps(self):
        for (what, k), (bank, n) in zip(self.plan, self.at):
            yield what, k, bank, (self.base[bank] + n if bank is not None else None)

    def value(self, step):
        bank, n = self.at[self.plan.index(step)]
        return bank, self.base[bank] + n

    def after(self, times=1):
        return [b + times * c for b, c in zip(self.base, self.count)]


def looped(plan, i, banks, uses, before=None):
    placed = Placed(plan, [0] * banks, uses)
    placed.base = [b + i * c for b, c in zip(before or [0] * banks, placed.count)]
    return placed


PRO = Placed(PROLOGUE, [0] * RING)
MID = Placed(PLAN, PRO.after())
SIX = Placed(PLAN_6, MID.after(6))
SEVEN = Placed(PLAN_7, SIX.after())


def iteration(i):
    return looped(PLAN, i, RING, TRANSPOSES + ("mx",), PRO.after())


def attention_stage(nc, a, G, y_sb):
    sc = Scope(nc, "att")
    sb, ps, sem = sc.sb, sc.ps, sc.sem
    G.causal_masks(sc)
    q_sb = y_sb
    k_sb = sb("k", [P, B * KVH, TB, HD])
    v_sb = sb("v", [P, B * KVH, TB, 32])

    pj = Scope(nc, "proj")
    xTb = pj.sb("xTb", [P, KD, S])
    wqkv = pj.sb("wqkv", [P, KD, 384])
    cos = pj.sb("cos", [P, TB, HD])
    sin = pj.sb("sin", [P, TB, HD])
    tcos = pj.sb("tcos", [P, 2, 20, HD])
    tsin = pj.sb("tsin", [P, 2, 20, HD])
    PQ = pj.ps("PQ", [P, 2, 512])
    x_in, w_in, c_in = pj.sem("x_in"), pj.sem("w_in"), pj.sem("c_in")
    qkv_ready, v_read = pj.sem("qkv_ready"), pj.sem("v_read")
    parts_ready, rope_done, v_blank = pj.sem("parts_ready"), pj.sem("rope_done"), pj.sem("v_blank")
    with nc.Block() as block:

        @block.sync
        def _(sp):
            sp.dma_start(xTb[:, :, :], a["xT"][:, :, 0:S]).then_inc(x_in, 16)
            sp.dma_start(wqkv[:, :, :], a["Wqkv"]).then_inc(w_in, 16)
            sp.dma_start(cos[:, :, :], a["cos"]).then_inc(c_in, 16)
            sp.dma_start(sin[:, :, :], a["sin"]).then_inc(c_in, 16)
            sp.dma_start(G.x_sb[:, :, :], a["x"]).then_inc(G.x_loaded, 16)
            sp.wait_ge(qkv_ready, TB)
            sp.dma_start(xTb[:, :, :], a["xT"][:, :, S:T]).then_inc(x_in, 16)

        @block.gpsimd
        def _(pool):
            pool.memset(v_sb[:, :, :, :], 0.0).then_inc(v_blank, 1)
            pool.wait_ge(v_blank, 1)
            pool.memset(v_sb[:, :, :, HD:HD + 1], 1.0).then_inc(v_blank, 1)
            G.constants(pool)
            with pool.Fori(0, B) as b:
                for t in range(TB):
                    pool.wait_ge(parts_ready, TB * b + t + 1)
                    by_group = [m[:, t % 2, 0:NH, :].rearrange("p (g r) d -> p g (r d)", g=KVH) for m in (tcos, tsin)]
                    pool.tensor_tensor(q_sb[:, ds(KVH * b, KVH), t, :], by_group[0], by_group[1], ALU.add)
                    last = pool.tensor_tensor(k_sb[:, ds(KVH * b, KVH), t, :], tcos[:, t % 2, NH:NH + KVH, :],
                                              tsin[:, t % 2, NH:NH + KVH, :], ALU.add)
                    last.then_inc(rope_done, 1)

        @block.scalar
        def _(act):
            act.sem_inc(v_read, 2)
            act.wait_ge(v_blank, 2)
            with act.Fori(0, B) as b:
                for t in range(TB):
                    act.wait_ge(parts_ready, TB * b + t + 1)
                    act.activation(v_sb[:, ds(KVH * b, KVH), t, 0:HD],
                                   PQ[:, t % 2, 320:384].rearrange("p (g d) -> p g d", d=HD),
                                   ACT.Copy).then_inc(v_read, 1)

        @block.vector
        def _(dve):
            dve.sem_inc(rope_done, 2)
            dve.wait_ge(c_in, 32)
            with dve.Fori(0, B) as b:
                for t in range(TB):
                    qk = PQ[:, t % 2, 0:320].rearrange("p (h d) -> p h d", d=HD)
                    c, s = bcast(cos[:, t, :], 1, 20), bcast(sin[:, t, :], 1, 20)
                    dve.wait_ge(qkv_ready, TB * b + t + 1)
                    dve.wait_ge(rope_done, TB * b + t + 1)
                    dve.tensor_tensor(tcos[:, t % 2, :, :], qk, c, ALU.mult)
                    dve.tensor_tensor(tsin[:, t % 2, :, 0:8], qk[:, :, 8:16], s[:, :, 0:8], ALU.mult)
                    dve.tensor_tensor(tsin[:, t % 2, :, 8:16], qk[:, :, 0:8], s[:, :, 8:16],
                                      ALU.mult).then_inc(parts_ready, 1)

        @block.tensor
        def _(pe):
            pe.wait_ge(w_in, 16)
            with pe.Fori(0, B) as b:
                pe.wait_ge(x_in, 16 * b + 16)
                for t in range(TB):
                    pe.wait_ge(v_read, TB * b + t + 1)
                    for kk in range(KD):
                        mm = pe.matmul(PQ[:, t % 2, 0:384], xTb[:, kk, t * P:(t + 1) * P], wqkv[:, kk, :],
                                       start=(kk == 0), stop=(kk == KD - 1))
                    mm.then_inc(qkv_ready, 1)
    pj.close(G.spent)

    qst = [sb(f"qst{p}", [P, TB, REP, P], BF16) for p in range(2)]
    kst = [sb(f"kst{p}", [P, TB, P], BF16) for p in range(2)]
    qT = [sb(f"qT{p}", [P, REP, S], BF16) for p in range(2)]
    kT = [sb(f"kT{p}", [P, S], BF16) for p in range(2)]
    vst = [sb(f"vst{p}", [P, TB, 32]) for p in range(2)]
    rest_q = [sb(f"rest_q{p}", [P, TB, REP, HD]) for p in range(2)]
    rest_k = [sb(f"rest_k{p}", [P, TB, HD]) for p in range(2)]
    rest_m = sb("rest_m", [P, TB, REP])
    negm = sb("negm", [P, TB, REP])
    rowmax = sb("rowmax", [P, TB, REP])
    mx = [sb(f"mx{p}", [P, TB, REP, 2]) for p in range(2)]
    junk = sb("junk", [P, RING, 512])
    PT = [sb(f"PT{p}", [P, 2, 512]) for p in range(4)]
    oT = [sb(f"oT{p}", [P, 512]) for p in range(2)]
    rden = [sb(f"rden{p}", [P, 4, REP]) for p in range(2)]
    RB = ps("RB", [P, RING, 512])
    RBb = [RB[:, n, :].bitcast(BF16) for n in range(RING)]
    ST = ps("ST", [P, 4, 512])
    OT = ps("OT", [P, 512])

    blanked = sem("blanked")
    stack_ready, stack0_ready = sem("stack_ready"), sem("stack0_ready")
    v_ready, negm_ready = sem("v_ready"), sem("negm_ready")
    bank_ready = [sem(f"bank_ready{n}") for n in range(RING)]
    bank_free = [sem(f"bank_free{n}") for n in range(RING)]
    row_done = sem("row_done")
    st_ready, exp_done, pv_done = sem("st_ready"), sem("exp_done"), sem("pv_done")
    ot_copied = sem("ot_copied")
    pool_chain, dve_chain = sem("pool_chain"), sem("dve_chain")

    EXP_CREDIT, PV_CREDIT, OT_CREDIT = 2, 4, 1

    def build(eng, ch, i, p, ready):
        q = q_sb[:, ds(i, 1), :, :].rearrange("p o t (r d) -> p (o t) r d", d=HD)
        k = k_sb[:, ds(i, 1), :, :].rearrange("p o t d -> p (o t) d")
        qs = lambda n: qst[p][:, :, :, n * HD:(n + 1) * HD]
        ks = lambda n: kst[p][:, :, n * HD:(n + 1) * HD]
        ch.done(eng.tensor_copy(qs(0), q))
        ch.done(eng.tensor_copy(ks(0), k))
        ch.wait()
        ch.done(eng.tensor_tensor(rest_q[p][:, :, :, :], q, qs(0), ALU.subtract))
        ch.done(eng.tensor_tensor(rest_k[p][:, :, :], k, ks(0), ALU.subtract))
        ch.wait()
        ch.done(eng.tensor_copy(qs(2), rest_q[p][:, :, :, :]))
        ch.done(eng.tensor_copy(ks(1), rest_k[p][:, :, :]))
        ch.wait()
        ch.done(eng.tensor_tensor(qs(5), rest_q[p][:, :, :, :], qs(2), ALU.subtract))
        ch.done(eng.tensor_tensor(ks(4), rest_k[p][:, :, :], ks(1), ALU.subtract))
        eng.tensor_copy(qs(1), qs(0))
        eng.tensor_copy(qs(4), qs(0))
        eng.tensor_copy(qs(3), qs(2))
        eng.tensor_copy(ks(2), ks(0))
        eng.tensor_copy(ks(5), ks(0))
        eng.tensor_copy(ks(3), ks(1)).then_inc(ready, 1)

    def buf_of(p, k):
        return p if k == 0 else 1 - p

    with nc.Block() as block:

        @block.sync
        def _(sp):
            G.prefetch_up(sp)

        @block.gpsimd
        def _(pool):
            ch = Chain(pool, pool_chain, G.passed)

            BUILD = 8

            def copy_v(i, p):
                pool.tensor_copy(vst[p][:, :, :], v_sb[:, ds(i, 1), :, :].rearrange("p o t d -> p (o t) d")
                                 ).then_inc(v_ready, 1)

            def negate_max(p):
                m = lambda n: qst[p][:, :, :, MROW + n]
                ch.link(pool.tensor_scalar(negm[:, :, :], rowmax[:, :, :], -1.0, None, ALU.mult))
                ch.link(pool.tensor_copy(m(0), negm[:, :, :]))
                ch.link(pool.tensor_tensor(rest_m[:, :, :], negm[:, :, :], m(0), ALU.subtract))
                ch.link(pool.tensor_copy(m(1), rest_m[:, :, :]))
                pool.tensor_tensor(m(2), rest_m[:, :, :], m(1), ALU.subtract).then_inc(negm_ready, 1)

            NEGATE = 4

            for p in range(2):
                pool.memset(qst[p][:, :, :, MROW:P], 0.0)
                pool.memset(kst[p][:, :, MROW + 3:P], 0.0)
                pool.memset(kst[p][:, :, MROW:MROW + 3], 1.0)
                last = pool.memset(mx[p][:, :, :, :], LOWEST)
            last.then_inc(blanked, 1)
            pool.wait_ge(blanked, 1)
            copy_v(0, 0)
            build(pool, ch, 1, 1, stack_ready)
            pool.wait_ge(row_done, 1)
            negate_max(0)

            def step(i, p, ahead):
                if ahead:
                    for bank in range(RING):
                        pool.wait_ge(bank_ready[bank], iteration(i).base[bank])
                    build(pool, ch, i + 2, p, stack_ready)
                pool.wait_ge(pv_done, NU * i + PV_CREDIT)
                copy_v(i + 1, 1 - p)
                pool.wait_ge(row_done, i + 2)
                settle(pool, G.passed)
                negate_max(1 - p)

            with pool.Fori(0, 3) as n:
                ch.enter(n, 2 * (BUILD + NEGATE))
                for u in range(2):
                    step(2 * n + u, u, True)
                ch.leave(3)
            step(6, 0, False)

        @block.scalar
        def _(act):
            act.sem_inc(exp_done, EXP_CREDIT)
            act.sem_inc(ot_copied, OT_CREDIT)

            def step(i, p, placed):
                for what, k, bank, value in placed.steps():
                    if what == "trm" and k % 2 == 0:
                        act.wait_ge(bank_ready[bank], value)
                        act.activation(qT[1 - p][MROW:P, k, :], RBb[bank][MROW:P, :],
                                       ACT.Copy).then_inc(bank_free[bank], 1)
                    if what == "trK":
                        act.wait_ge(bank_ready[bank], value)
                        act.activation(kT[buf_of(p, k)][:, :], RBb[bank], ACT.Copy).then_inc(bank_free[bank], 1)
                    if what == "trQ":
                        act.wait_ge(bank_ready[bank], value)
                        act.activation(qT[buf_of(p, k)][0:MROW, k % REP, :], RBb[bank][0:MROW, :],
                                       ACT.Copy).then_inc(bank_free[bank], 1)
                    if what == "st":
                        c, kt, pr = UNITS[k]
                        w = 512 - P * max(0, kt - 4 * c)
                        act.wait_ge(st_ready, NU * i + k + 1)
                        act.wait_ge(pv_done, NU * i + k + 1)
                        buf = PT[k % 4]
                        act.activation(buf[:, :, 0:w], ST[:, 2 * (k % 2):2 * (k % 2) + 2, 0:w], ACT.Exp,
                                       scale=float(HD) ** -0.5).then_inc(exp_done, 1)
                    if what == "otr":
                        act.wait_ge(pv_done, NU * i + (8, NU)[k] + PV_CREDIT)
                        for b in range(RING):
                            act.wait_ge(bank_ready[b], placed.base[b])
                        act.activation(oT[k][:, :], OT[:, :], ACT.Copy).then_inc(ot_copied, 1)

            step(-1, 1, PRO)
            with act.Fori(0, 3) as n:
                for u in range(2):
                    step(2 * n + u, u, iteration(2 * n + u))
            step(6, 0, SIX)
            step(7, 1, SEVEN)

        @block.vector
        def _(dve):
            ch = Chain(dve, dve_chain)
            dve.sem_inc(pv_done, PV_CREDIT)
            dve.wait_ge(blanked, 1)
            build(dve, ch, 0, 0, stack0_ready)

            def step(i, p, placed):
                for what, k, bank, value in placed.steps():
                    if what == "trm" and k % 2 == 1:
                        dve.wait_ge(bank_ready[bank], value)
                        dve.tensor_copy(qT[1 - p][MROW:P, k, :], RBb[bank][MROW:P, :]).then_inc(bank_free[bank], 1)
                    if what == "mx":
                        r, t, c = MAXES[k]
                        dve.wait_ge(bank_ready[bank], value)
                        if c == t // 4:
                            settle(dve, G.passed)
                        to = mx[1 - p][:, t, r, c:c + 1]
                        if c == t // 4:
                            w = (t % 4 + 1) * P
                            dve.tensor_tensor_reduce(junk[:, k % RING, 0:w], RB[:, bank, 0:w],
                                                     G.causal_q[:, 512 - w:512], 1.0, LOWEST, ALU.add, ALU.max,
                                                     to).then_inc(bank_free[bank], 1)
                        else:
                            dve.tensor_reduce(to, RB[:, bank, :], AX_X, ALU.max).then_inc(bank_free[bank], 1)
                        if k == NM - 1:
                            for n in (NM - 3, NM - 2, NM - 1):
                                dve.wait_ge(bank_free[placed.value(("mx", n))[0]], placed.value(("mx", n))[1])
                            dve.tensor_tensor(rowmax[:, :, :], mx[1 - p][:, :, :, 0], mx[1 - p][:, :, :, 1],
                                              ALU.max).then_inc(row_done, 1)
                    if what == "otr":
                        dve.wait_ge(bank_ready[bank], value)
                        o = RB[:, bank, :].rearrange("p (t r d) -> p t r d", t=4, d=32)
                        ch.link(dve.reciprocal(rden[k][:, :, :], o[:, :, :, HD]))
                        y = y_sb[:, ds(i, 1), 4 * k:4 * k + 4, :].rearrange("p o t (r d) -> p (o t) r d", d=HD)
                        dve.tensor_tensor(y, o[:, :, :, 0:HD], bcast(rden[k][:, :, :], 3, HD),
                                          ALU.mult).then_inc(bank_free[bank], 1)

            step(-1, 1, PRO)
            with dve.Fori(0, 3) as n:
                ch.enter(n, 4)
                for u in range(2):
                    step(2 * n + u, u, iteration(2 * n + u))
                ch.leave(3)
            step(6, 0, SIX)
            step(7, 1, SEVEN)

        @block.tensor
        def _(pe):
            def step(i, p, placed):
                front, ident = i + 1, G.ident_b
                for what, k, bank, value in placed.steps():
                    if bank is not None and not (isinstance(value, int) and value == 1):
                        pe.wait_ge(bank_free[bank], value - 1)
                    if what == "trm":
                        if k == 0:
                            pe.wait_ge(negm_ready, front + 1)
                        for t in range(TB):
                            mm = pe.transpose(RBb[bank][MROW:P, t * P:(t + 1) * P], qst[1 - p][:, t, k, MROW:P], ident[:, :])
                        mm.then_inc(bank_ready[bank], 1)
                    if what == "trK":
                        if k < 0:
                            pe.wait_ge(stack0_ready, 1)
                        else:
                            pe.wait_ge(stack_ready, front + 1)
                        for t in range(TB):
                            mm = pe.transpose(RBb[bank][:, t * P:(t + 1) * P], kst[buf_of(p, k)][:, t, :], ident[:, :])
                        mm.then_inc(bank_ready[bank], 1)
                    if what == "trQ":
                        for t in range(TB):
                            mm = pe.transpose(RBb[bank][0:MROW, t * P:(t + 1) * P],
                                              qst[buf_of(p, k)][:, t, k % REP, 0:MROW], ident[:, :])
                        mm.then_inc(bank_ready[bank], 1)
                    if what == "mx":
                        r, t, c = MAXES[k]
                        w = P * (t % 4 + 1) if c == t // 4 else 512
                        if k % 12 == 0 and ("trQ", r or -REP) in placed.plan:
                            b, v = placed.value(("trQ", r or -REP))
                            pe.wait_ge(bank_free[b], v)
                        if k == 0:
                            for b in range(RING):
                                if not isinstance(placed.base[b], int) or placed.base[b] > 0:
                                    pe.wait_ge(bank_free[b], placed.base[b])
                        pe.matmul(RB[:, bank, 0:w], qT[1 - p][0:MROW, r, t * P:(t + 1) * P],
                                  kT[1 - p][0:MROW, 512 * c:512 * c + w], start=True, stop=True).then_inc(bank_ready[bank], 1)
                    if what == "st":
                        c, kt, pr = UNITS[k]
                        off = P * max(0, kt - 4 * c)
                        diag = kt >= 4 * c
                        if k == 0:
                            for b in range(RING):
                                pe.wait_ge(bank_free[b], placed.base[b] - (placed is not SEVEN))
                        pe.wait_ge(exp_done, NU * i + k + 1)
                        for h in range(2):
                            r = 2 * pr + h
                            to = ST[:, 2 * (k % 2) + h, :]
                            mm = pe.matmul(to[:, 0:512 - off], kT[p][:, kt * P:(kt + 1) * P],
                                           qT[p][:, r, 512 * c + off:512 * c + 512], start=True, stop=not diag)
                            if diag:
                                mm = pe.matmul(to[:, 0:P], ident[:, :], G.causal_k[:, :], start=False, stop=True)
                        mm.then_inc(st_ready, 1)
                    if what == "pv":
                        c, kt, pr = UNITS[k]
                        off = P * max(0, kt - 4 * c)
                        if k == 0:
                            pe.wait_ge(v_ready, i + 1)
                        if kt == 0 and pr == 0:
                            pe.wait_ge(ot_copied, 2 * i + c + 1)
                        pe.wait_ge(exp_done, NU * i + k + 1 + EXP_CREDIT)
                        for h in range(2):
                            r = 2 * pr + h
                            mm = pe.matmul(OT[32 * r:32 * r + 32, off:512], vst[p][:, kt, :],
                                           PT[k % 4][:, h, 0:512 - off], start=(kt == 0), stop=(kt == 4 * c + 3))
                        mm.then_inc(pv_done, 1)
                    if what == "otr":
                        pe.wait_ge(ot_copied, 2 * i + k + 1 + OT_CREDIT)
                        for t in range(4):
                            mm = pe.transpose(RB[:, bank, t * P:(t + 1) * P], oT[k][:, t * P:(t + 1) * P], G.ident_f[:, :])
                        mm.then_inc(bank_ready[bank], 1)

            pe.wait_ge(G.const_ready, G.CONSTS)
            step(-1, 1, PRO)
            with pe.Fori(0, 3) as n:
                for u in range(2):
                    step(2 * n + u, u, iteration(2 * n + u))
            step(6, 0, SIX)
            step(7, 1, SEVEN)
    sc.close(G.spent)


def xattn_stage(nc, a, G, y_sb):
    sc = Scope(nc, "xa")
    sb, ps, sem = sc.sb, sc.ps, sc.sem
    NB = 8
    J = 4
    SK = 64
    HH = NH // 2
    wo = sb("wo", [P, KD, D])
    wx_f = sb("wx_f", [P, 4, KD, D])
    wx = sb("wx", [P, 4, KD, D], BF16)
    cT_f = sb("cT_f", [P, KD, B * SK])
    cT = sb("cT", [P, KD, B * SK], BF16)
    cT2 = sb("cT2", [P, KD, B, 2, SK], BF16)
    bcol_f = sb("bcol_f", [P, 2, KD])
    bcol_b = sb("bcol_b", [P, 2, KD], BF16)
    bcol = sb("bcol", [P, 2, KD])
    brow_f = sb("brow_f", [P, 2, D])
    brow = sb("brow", [P, 2, D], BF16)
    m_i = sb("m_i", [P, B, SK], I32)
    m_f = sb("m_f", [P, B, SK])
    mask = sb("mask", [P, NT, SK], BF16)
    bd = sb("bd", [P, HH], BF16)
    k0 = sb("k0", [P, KD, B * SK], BF16)
    k1 = sb("k1", [P, KD, B * SK], BF16)
    KBD = sb("KBD", [P, B, KD, HH, SK], BF16)
    v0 = sb("v0", [P, B, D], BF16)
    v1 = sb("v1", [P, B, D], BF16)
    VW = HD + 1
    VBD = sb("VBD", [P, B, HH, 2 * VW])
    ys = sb("ys", [P, J, D])
    yT = sb("yT", [P, J, KD, P])
    xr = sb("xr", [P, J, D])
    st = sb("st", [P, J, 6])
    mv = sb("mv", [P, J, 2])
    rstd = sb("rstd", [P, J])
    half = sb("half", [P, J])
    xb = sb("xb", [P, J, D], BF16)
    xbT = sb("xbT", [P, KD, J * P], BF16)
    q0 = sb("q0", [P, KD, J * P], BF16)
    q1 = sb("q1", [P, KD, J * P], BF16)
    mxs = sb("mxs", [P, J, NH])
    sub = sb("sub", [P, 2, HH, SK])
    pr = sb("pr", [P, J, NH * SK])
    pT = sb("pT", [P, J, 2, 4, P])
    rd = sb("rd", [P, J, NH])
    yb = sb("yb", [P, J, D], BF16)
    ybT = sb("ybT", [P, J, KD, P], BF16)
    o0 = sb("o0", [P, J, D], BF16)
    o1 = sb("o1", [P, J, D], BF16)
    R = ps("R", [P, NB, 512])
    Rb = [R[:, n, :].bitcast(BF16) for n in range(NB)]
    ready = [sem(f"bank_ready{n}") for n in range(NB)]
    free = [sem(f"bank_free{n}") for n in range(NB)]
    w_in, cast_a, cast_d = sem("w_in"), sem("cast_a"), sem("cast_d")
    pool_set, k_set, v_set = sem("pool_set"), sem("k_set"), sem("v_set")
    ys_ready, var_ready, rstd_ready = sem("ys_ready"), sem("var_ready"), sem("rstd_ready")
    x1_ready, xb_ready, q_ready = sem("x1_ready"), sem("xb_ready"), sem("q_ready")
    exp_done = sem("exp_done")
    o0_ready = sem("o0_ready")
    c_dve, c_act, c_pool = sem("c_dve"), sem("c_act"), sem("c_pool")
    ys_read = sem("ys_read")
    LOADS = 9

    SETUP = [("k", 0), ("k", 1), ("v", 0), ("v", 1)]
    PLAN = []
    for what in ("ty", "wo", "tx"):
        PLAN += [(what, j) for j in range(J)]
    PLAN += [("q", m) for m in range(KD)]
    PLAN += [("s", n) for n in range(2 * J)]
    for what, n in (("tp", 2 * J), ("pv", J), ("tb", J), ("ox", J)):
        PLAN += [(what, j) for j in range(n)]
    USES = ("k", "v", "ty", "wo", "tx", "q", "s", "tp", "pv", "tb", "ox")
    setup = Placed(SETUP, [0] * NB, USES)

    def iteration(i):
        return looped(PLAN, i, NB, USES, setup.after())

    with nc.Block() as block:

        @block.sync
        def _(sp):
            sp.dma_start(wo[:, :, :], a["Wo"]).then_inc(w_in, 16)
            sp.dma_start(wx_f[:, :, :, :], a["WX"]).then_inc(w_in, 16)
            sp.dma_start(cT_f[:, :, :], a["ctxT"]).then_inc(w_in, 16)
            sp.dma_start(bcol_f[:, 0, :], a["bq"]).then_inc(w_in, 16)
            sp.dma_start(bcol_f[:, 1, :], a["bk"]).then_inc(w_in, 16)
            sp.dma_start(brow_f[:, 0, :], a["bv"].partition_broadcast(P)).then_inc(w_in, 16)
            sp.dma_start(brow_f[:, 1, :], a["bo"].partition_broadcast(P)).then_inc(w_in, 16)
            sp.dma_start(m_i[:, :, :], a["mask0"].partition_broadcast(P)).then_inc(w_in, 16)
            sp.wait_ge(G.x_loaded, 16)
            sp.sem_inc(w_in, 16)

        @block.gpsimd
        def _(pool):
            ch = Chain(pool, c_pool, G.passed)
            ch.link(pool.memset(bd[:, :], 1.0))
            ch.link(pool.affine_select(out=bd[:, :], in_=bd[:, :], compare_op=ALU.is_ge, fill=0.0, base=0,
                                       pattern=[[-HD, HH]], channel_multiplier=1))
            pool.affine_select(out=bd[:, :], in_=bd[:, :], compare_op=ALU.is_ge, fill=0.0, base=HD - 1,
                               pattern=[[HD, HH]], channel_multiplier=-1)
            pool.memset(half[:, :], -0.5)
            ch.link(pool.memset(VBD[:, :, :, :], 0.0))
            ch.link(pool.memset(VBD[0:SK, :, :, HD:HD + 1], 1.0))
            pool.memset(VBD[SK:P, :, :, VW + HD:VW + HD + 1], 1.0).then_inc(pool_set, 1)
            pool.wait_ge(pool_set, 1)
            pool.wait_ge(w_in, 16 * LOADS)
            ch.link(pool.tensor_scalar(m_f[:, :, :], m_i[:, :, :], 0.0, None, ALU.is_gt))
            ch.link(pool.tensor_scalar(m_f[:, :, :], m_f[:, :, :], -1.0, -NEG, ALU.add, ALU.mult))
            for b in range(B):
                n = pool.tensor_copy(mask[:, b * TB:(b + 1) * TB, :], bcast(m_f[:, b, :], 1, TB))
            ch.link(n)
            for b in range(B):
                n = pool.affine_select(out=mask[:, b * TB, :], in_=mask[:, b * TB, :], compare_op=ALU.is_ge, fill=NEG,
                                       base=0, pattern=[[-1, SK]], channel_multiplier=1)
            n.then_inc(pool_set, 1)
            with pool.Fori(0, NT // J) as i:
                ch.enter(i, 2)
                for j in range(J):
                    pool.wait_ge(ys_read, J * i + j + 1)
                    pool.tensor_copy(ys[:, j, :].rearrange("p (g c) -> p g c", g=KVH),
                                     y_sb[:, ds(KVH * (i // 2), KVH), ds(J * (i % 2) + j, 1), :]
                                     .rearrange("p g o c -> p g (o c)")).then_inc(ys_ready, 1)
                for k in range(2):
                    pool.wait_ge(var_ready, 2 * i + k + 1)
                    settle(pool, G.passed)
                    ch.link(pool.tensor_scalar(rstd[:, :], mv[:, :, 1], LN_EPS, None, ALU.add))
                    pool.tensor_tensor(rstd[:, :], rstd[:, :], half[:, :], ALU.pow).then_inc(rstd_ready, 1)
                ch.leave(NT // J)

        @block.scalar
        def _(act):
            ch = Chain(act, c_act)
            act.wait_ge(w_in, 16 * LOADS)
            act.activation(cT[:, :, :], cT_f[:, :, :], ACT.Copy)
            act.activation(wx[:, 1, :, :], wx_f[:, 1, :, :], ACT.Copy).then_inc(cast_a, 1)
            act.activation(wx[:, 0, :, :], wx_f[:, 0, :, :], ACT.Copy)
            act.activation(wx[:, 3, :, :], wx_f[:, 3, :, :], ACT.Copy).then_inc(cast_a, 1)
            act.wait_ge(cast_d, 1)
            for what, m, bank, value in setup.steps():
                act.wait_ge(ready[bank], value)
                if what == "k":
                    ch.link(act.activation(k0[:, m, :], R[:, bank, 0:B * SK], ACT.Copy))
                    act.activation(k1[:, m, :], k0[:, m, :], ACT.Identity, bias=bcol[:, 1, m:m + 1]).then_inc(k_set, 1)
                else:
                    act.activation(v0[:, m, :], R[:, bank, 0:D], ACT.Copy).then_inc(v_set, 1)
            with act.Fori(0, NT // J) as i:
                for what, k, bank, value in iteration(i).steps():
                    j = k
                    if what == "ty":
                        act.wait_ge(ready[bank], value)
                        act.activation(yT[:, j, :, :], R[:, bank, 0:D].rearrange("p (k c) -> p k c", k=KD),
                                       ACT.Copy).then_inc(free[bank], 1)
                    if what == "tx":
                        act.wait_ge(x1_ready, J * i + j + 1)
                        act.activation(xb[:, j, :], G.x_sb[:, ds(J * i + j, 1), :].rearrange("p o c -> p (o c)"),
                                       ACT.Copy).then_inc(xb_ready, 1)
                for what, k, bank, value in iteration(i).steps():
                    j = k
                    if what == "tx":
                        act.wait_ge(ready[bank], value)
                        act.activation(xbT[:, :, j * P:(j + 1) * P],
                                       Rb[bank][:, 0:D].rearrange("p (k c) -> p k c", k=KD),
                                       ACT.Copy).then_inc(free[bank], 1)
                    if what == "q":
                        act.wait_ge(ready[bank], value)
                        act.activation(q0[:, k, :], R[:, bank, :], ACT.Copy).then_inc(free[bank], 1)
                        act.wait_ge(free[bank], value + 1)
                        act.activation(q1[:, k, :], q0[:, k, :], ACT.Identity,
                                       bias=bcol[:, 0, k:k + 1]).then_inc(q_ready, 1)
                    if what == "s":
                        act.wait_ge(free[bank], value + 1)
                        act.activation(pr[:, k // 2, 512 * (k % 2):512 * (k % 2) + 512],
                                       sub[:, k % 2, :, :].rearrange("p h c -> p (h c)"), ACT.Exp,
                                       scale=float(HD) ** -0.5).then_inc(exp_done, 1)
                    if what == "tp":
                        act.wait_ge(ready[bank], value)
                        act.activation(pT[:, k // 2, k % 2, :, :], R[:, bank, :].rearrange("p (m c) -> p m c", c=P),
                                       ACT.Copy).then_inc(free[bank], 1)
                    if what == "tb":
                        act.wait_ge(ready[bank], value)
                        act.activation(ybT[:, j, :, :], Rb[bank][:, 0:D].rearrange("p (k c) -> p k c", k=KD),
                                       ACT.Copy).then_inc(free[bank], 1)
                    if what == "ox":
                        act.wait_ge(ready[bank], value)
                        act.activation(o0[:, j, :], R[:, bank, 0:D], ACT.Copy).then_inc(free[bank], 1)

        @block.vector
        def _(dve):
            ch = Chain(dve, c_dve)
            dve.wait_ge(w_in, 16 * LOADS)
            ch.done(dve.tensor_copy(bcol_b[:, :, :], bcol_f[:, :, :]))
            ch.done(dve.tensor_copy(brow[:, :, :], brow_f[:, :, :]))
            ch.wait()
            dve.tensor_copy(wx[:, 2, :, :], wx_f[:, 2, :, :])
            dve.tensor_copy(bcol[:, :, :], bcol_b[:, :, :]).then_inc(cast_d, 1)
            dve.wait_ge(cast_a, 1)
            for kk in range(KD):
                n = dve.tensor_copy(cT2[:, kk, :, :, :].rearrange("p b u c -> p b u c"),
                                    bcast(cT[:, kk, :].rearrange("p (b c) -> p b c", b=B), 2, 2))
            n.then_inc(cast_d, 1)
            dve.wait_ge(k_set, KD)
            dve.wait_ge(pool_set, 2)
            for b in range(B):
                for m in range(KD):
                    kt = bcast(k1[:, m, b * SK:(b + 1) * SK], 1, HH)
                    ch.done(dve.tensor_tensor(KBD[:, b, m, :, :], kt, bcast(bd[:, :], 2, SK), ALU.mult))
            dve.wait_ge(v_set, B)
            ch.link(dve.tensor_tensor(v1[:, :, :], v0[:, :, :], bcast(brow[:, 0, :], 1, B), ALU.add))
            for b in range(B):
                v = v1[:, b, :].rearrange("p (m u d) -> p m u d", u=2, d=HD)
                ch.done(dve.tensor_copy(VBD[0:SK, b, :, 0:HD], v[0:SK, :, 0, :]))
                ch.done(dve.tensor_copy(VBD[SK:P, b, :, VW:VW + HD], v[SK:P, :, 1, :]))
            ch.wait()
            dve.sem_inc(cast_d, 1)
            for n in range(NB):
                dve.sem_inc(free[n], 1 + setup.count[n])
            dve.sem_inc(exp_done, 2)
            dve.sem_inc(G.x2_ready, 1)
            dve.sem_inc(ys_read, J)

            def norm(i, k):
                n = [ch.done(dve.bn_stats(st[:, j, :], xr[:, j, :])) for j in range(J)]
                for j in range(J):
                    ch.wait(n[j])
                    settle(dve, G.passed)
                    last = dve.bn_aggr(mv[:, j, :], st[:, j, :])
                last.then_inc(var_ready, 1)
                dve.wait_ge(rstd_ready, 2 * i + k + 1)
                for j in range(J):
                    last = dve.tensor_scalar(G.x_sb[:, ds(J * i + j, 1), :].rearrange("p o c -> p (o c)"),
                                             xr[:, j, :], mv[:, j, 0:1], rstd[:, j:j + 1], ALU.subtract, ALU.mult)
                    last.then_inc(x1_ready if k == 0 else G.x2_ready, 1)

            with dve.Fori(0, NT // J) as i:
                ch.enter(i, 7 * J)
                placed = iteration(i)
                x_of = lambda j: G.x_sb[:, ds(J * i + j, 1), :].rearrange("p o c -> p (o c)")
                for what, k, bank, value in placed.steps():
                    j = k
                    if what == "wo":
                        if j == 0:
                            dve.wait_ge(G.x2_ready, J * i + 1)
                        dve.wait_ge(ready[bank], value)
                        dve.tensor_tensor(xr[:, j, :], R[:, bank, 0:D], x_of(j), ALU.add).then_inc(free[bank], 1)
                        if j == J - 1:
                            for jj in range(J):
                                b, v = placed.value(("wo", jj))
                                dve.wait_ge(free[b], v + 1)
                            norm(i, 0)
                    if what == "s":
                        dve.wait_ge(ready[bank], value)
                        dve.wait_ge(exp_done, 2 * J * i + k + 1)
                        sc3 = R[:, bank, :].rearrange("p (h c) -> p h c", c=SK)
                        top = mxs[:, j // 2, HH * (k % 2):HH * (k % 2) + HH]
                        ch.link(dve.tensor_reduce(top, sc3, AX_X, ALU.max))
                        dve.tensor_tensor(sub[:, k % 2, :, :], sc3, bcast(top, 2, SK), ALU.subtract
                                          ).then_inc(free[bank], 1)
                    if what == "pv":
                        dve.wait_ge(ready[bank], value)
                        o = R[:, bank, 0:HH * 2 * VW].rearrange("p (h d) -> p h d", d=VW)
                        ch.link(dve.reciprocal(rd[:, j, :], o[:, :, HD]))
                        dve.tensor_tensor(yb[:, j, :].rearrange("p (h d) -> p h d", d=HD), o[:, :, 0:HD],
                                          bcast(rd[:, j, :], 2, HD), ALU.mult).then_inc(free[bank], 1)
                    if what == "ox":
                        dve.wait_ge(free[bank], value + 1)
                        ch.link(dve.tensor_tensor(o1[:, j, :], o0[:, j, :], brow[:, 1, :], ALU.add))
                        ch.link(dve.tensor_tensor(xr[:, j, :], o1[:, j, :], x_of(j), ALU.add))
                        if j == J - 1:
                            norm(i, 1)
                ch.leave(NT // J)

        @block.tensor
        def _(pe):
            pe.wait_ge(cast_a, 1)
            pe.wait_ge(cast_d, 2)
            for what, m, bank, value in setup.steps():
                for kk in range(KD):
                    if what == "k":
                        mm = pe.matmul(R[:, bank, 0:B * SK], wx[:, 1, kk, m * P:(m + 1) * P], cT[:, kk, :],
                                       start=(kk == 0), stop=(kk == KD - 1))
                    else:
                        mm = pe.matmul(R[:, bank, 0:D], cT2[:, kk, m, :, :].rearrange("p u c -> p (u c)"), wx[:, 2, kk, :],
                                       start=(kk == 0), stop=(kk == KD - 1))
                mm.then_inc(ready[bank], 1)
            pe.wait_ge(cast_a, 2)
            pe.wait_ge(cast_d, 3)
            with pe.Fori(0, NT // J) as i:
                placed = iteration(i)
                b2 = i // 2
                for what, k, bank, value in placed.steps():
                    j = k
                    pe.wait_ge(free[bank], value)
                    if what == "ty":
                        pe.wait_ge(ys_ready, J * i + j + 1)
                        for kk in range(KD):
                            mm = pe.transpose(R[:, bank, kk * P:(kk + 1) * P], ys[:, j, kk * P:(kk + 1) * P], G.ident_f[:, :])
                    if what == "wo":
                        b, v = placed.value(("ty", j))
                        pe.wait_ge(free[b], v + 1)
                        for kk in range(KD):
                            mm = pe.matmul(R[:, bank, 0:D], yT[:, j, kk, :], wo[:, kk, :],
                                           start=(kk == 0), stop=(kk == KD - 1))
                    if what == "tx":
                        if j == 0:
                            pe.sem_inc(ys_read, J)
                        pe.wait_ge(xb_ready, J * i + j + 1)
                        for kk in range(KD):
                            mm = pe.transpose(Rb[bank][:, kk * P:(kk + 1) * P], xb[:, j, kk * P:(kk + 1) * P], G.ident_b[:, :])
                    if what == "q":
                        if k == 0:
                            for jj in range(J):
                                b, v = placed.value(("tx", jj))
                                pe.wait_ge(free[b], v + 1)
                        for kk in range(KD):
                            mm = pe.matmul(R[:, bank, :], wx[:, 0, kk, k * P:(k + 1) * P], xbT[:, kk, :],
                                           start=(kk == 0), stop=(kk == KD - 1))
                    if what == "s":
                        if k == 0:
                            pe.wait_ge(q_ready, KD * i + KD)
                        t, m = k // 2, k % 2
                        pe.matmul(R[:, bank, :], q1[:, m, t * P:(t + 1) * P],
                                  KBD[:, ds(b2, 1), m, :, :].rearrange("p o h c -> p (o h c)"), start=True, stop=False)
                        mm = pe.matmul(R[:, bank, :].rearrange("p (h c) -> p h c", c=SK), G.ident_b[:, :],
                                       mask[:, ds(J * i + t, 1), :].to_broadcast([P, HH, SK]), start=False, stop=True)
                    if what == "tp":
                        pe.wait_ge(exp_done, 2 * J * i + k + 3)
                        for m in range(4):
                            c = 512 * (k % 2) + m * P
                            mm = pe.transpose(R[:, bank, m * P:(m + 1) * P], pr[:, k // 2, c:c + P], G.ident_f[:, :])
                    if what == "pv":
                        for h in range(2):
                            b, v = placed.value(("tp", 2 * j + h))
                            pe.wait_ge(free[b], v + 1)
                        for m in range(HH):
                            mm = pe.matmul(R[:, bank, m * 2 * VW:(m + 1) * 2 * VW], pT[:, j, m // 4, m % 4, :],
                                           VBD[:, ds(b2, 1), m, :].rearrange("p o c -> p (o c)"), start=True, stop=True)
                    if what == "tb":
                        b, v = placed.value(("pv", j))
                        pe.wait_ge(free[b], v + 1)
                        for kk in range(KD):
                            mm = pe.transpose(Rb[bank][:, kk * P:(kk + 1) * P], yb[:, j, kk * P:(kk + 1) * P], G.ident_b[:, :])
                    if what == "ox":
                        b, v = placed.value(("tb", j))
                        pe.wait_ge(free[b], v + 1)
                        for kk in range(KD):
                            mm = pe.matmul(R[:, bank, 0:D], ybT[:, j, kk, :], wx[:, 3, kk, :],
                                           start=(kk == 0), stop=(kk == KD - 1))
                    mm.then_inc(ready[bank], 1)
    sc.close(G.spent)


class Mixture:

    def __init__(self, name, E, K, shared, first):
        self.name, self.E, self.K = name, E, K
        self.SHARED = shared
        self.FIRST, self.LAST = first, len(shared) - first
        full = T * K // P + E - 1
        self.ROUTED = full + (full + len(shared)) % 2
        self.ITEMS = self.ROUTED + len(shared)
        self.IDS = [e for e, _ in shared[:first]] + [None] * self.ROUTED + [e for e, _ in shared[first:]]

    def row_of_shared(self, n):
        return P * (n if n < self.FIRST else n + self.ROUTED)


MIX0 = Mixture("f0", 8, 2, [(8, t) for t in range(NT)], 8)
MIX1 = Mixture("f1", 16, 4, [(16, t) for t in range(NT)] + [(17, t) for t in range(NT)], NT)


def routing_stage(nc, a, G, M, gate, gate_bias, Xd, pos, wgt, ids, prefetch):
    sc = Scope(nc, M.name + "r")
    sb, ps, sem = sc.sb, sc.ps, sc.sem
    E, K, J, NB = M.E, M.K, 4, 8
    GR = 4
    wg = sb("wg", [P, KD, E])
    gb = sb("gb", [P, E])
    xs = sb("xs", [P, J, D])
    xT = sb("xT", [P, J, KD, P])
    sg = sb("sg", [P, NT, E])
    ma = sb("ma", [P, NT, E])
    cmp_a = sb("cmp_a", [P, NT * E * E], BF16)
    cmp_b = sb("cmp_b", [P, NT * E * E], BF16)
    low = sb("low", [P, E, E], BF16)
    upper = sb("upper", [P, P], BF16)
    ones = sb("ones", [P, P], BF16)
    one_f = sb("one_f", [P, NT])
    rank = sb("rank", [P, NT, E])
    grp = sb("grp", [P, NT, GR])
    grank = sb("grank", [P, NT, GR])
    sel = sb("sel", [P, NT, E], BF16)
    hot = sb("hot", [P, NT, E])
    incl = sb("incl", [P, NT, E])
    place = sb("place", [P, NT, E])
    steps = sb("steps", [P, NT])
    over = sb("over", [P, E, NT])
    tiles = sb("tiles", [P, E])
    ends = sb("ends", [P, E])
    starts = sb("starts", [P, E])
    posf = sb("posf", [P, NT, K])
    tot = sb("tot", [P, NT])
    item = sb("item", [1, M.ROUTED])
    past = sb("past", [1, M.ROUTED, E])
    idf = sb("idf", [1, M.ITEMS])
    R = ps("R", [P, NB, 512])
    ready = [sem(f"bank_ready{n}") for n in range(NB)]
    free = [sem(f"bank_free{n}") for n in range(NB)]
    w_in, stored = sem("w_in"), sem("stored")
    consts, xs_ready, xs_read = sem("consts"), sem("xs_ready"), sem("xs_read")
    exp_done, logits, sel_ready, sums_ready = sem("exp_done"), sem("logits"), sem("sel_ready"), sem("sums_ready")
    c_dve, c_pool = sem("c_dve"), sem("c_pool")
    PLAN = [("ty", j) for j in range(J)] + [("g", j) for j in range(J)]
    USES = ("ty", "g")

    with nc.Block() as block:

        @block.sync
        def _(sp):
            sp.dma_start(wg[:, :, :], gate).then_inc(w_in, 16)
            if gate_bias is not None:
                sp.dma_start(gb[:, :], gate_bias.partition_broadcast(P)).then_inc(w_in, 16)
            else:
                sp.sem_inc(w_in, 16)
            runs = [(0, M.FIRST), (M.FIRST, M.FIRST + M.LAST)]
            if len(M.SHARED) > NT:
                runs = [(n, n + NT) for n in range(0, len(M.SHARED), NT)]
            for n0, n1 in runs:
                row, t0 = M.row_of_shared(n0), M.SHARED[n0][1]
                sp.dma_start(Xd[row:row + P * (n1 - n0), :].rearrange("(t p) c -> p t c", p=P),
                             G.x_sb[:, t0:t0 + n1 - n0, :]).then_inc(stored, 16)
            prefetch(sp)
            sp.wait_ge(stored, 32)

        @block.gpsimd
        def _(pool):
            ch = Chain(pool, c_pool, G.passed)
            pool.memset(low[:, :, :], 1.0)
            pool.memset(ones[:, :], 1.0)
            pool.memset(one_f[:, :], 1.0)
            ch.link(pool.memset(upper[:, :], 1.0))
            pool.affine_select(out=low[:, :, :], in_=low[:, :, :], compare_op=ALU.is_gt, fill=0.0, base=0,
                               pattern=[[1, E], [-1, E]], channel_multiplier=0)
            pool.affine_select(out=upper[:, :], in_=upper[:, :], compare_op=ALU.is_gt, fill=0.0, base=0,
                               pattern=[[1, P]], channel_multiplier=-1)
            pool.iota(steps[:, :], pattern=[[P, NT]], base=0, channel_multiplier=0,
                      allow_small_or_imprecise_dtypes=True)
            pool.iota(item[:, :], pattern=[[1, M.ROUTED]], base=0, channel_multiplier=0,
                      allow_small_or_imprecise_dtypes=True).then_inc(consts, 1)
            with pool.Fori(0, NT // J) as i:
                for j in range(J):
                    pool.wait_ge(xs_read, J * i + j + 1)
                    pool.tensor_copy(xs[:, j, :], G.x_sb[:, ds(J * i + j, 1), :].rearrange("p o c -> p (o c)")
                                     ).then_inc(xs_ready, 1)

        @block.scalar
        def _(act):
            with act.Fori(0, NT // J) as i:
                for what, j, bank, value in looped(PLAN, i, NB, USES).steps():
                    if what == "ty":
                        act.wait_ge(ready[bank], value)
                        act.activation(xT[:, j, :, :], R[:, bank, 0:D].rearrange("p (k c) -> p k c", k=KD),
                                       ACT.Copy).then_inc(free[bank], 1)
            act.wait_ge(logits, NT)
            act.activation(hot[:, :, :], sg[:, :, :], ACT.Exp, scale=-1.0).then_inc(exp_done, 1)

        @block.tensor
        def _(pe):
            pe.wait_ge(w_in, 32)
            with pe.Fori(0, NT // J) as i:
                placed = looped(PLAN, i, NB, USES)
                for what, j, bank, value in placed.steps():
                    pe.wait_ge(free[bank], value)
                    if what == "ty":
                        pe.wait_ge(xs_ready, J * i + j + 1)
                        for kk in range(KD):
                            mm = pe.transpose(R[:, bank, kk * P:(kk + 1) * P], xs[:, j, kk * P:(kk + 1) * P], G.ident_f[:, :])
                    else:
                        b, v = placed.value(("ty", j))
                        pe.wait_ge(free[b], v + 1)
                        for kk in range(KD):
                            mm = pe.matmul(R[:, bank, 0:E], xT[:, j, kk, :], wg[:, kk, :],
                                           start=(kk == 0), stop=(kk == KD - 1))
                    mm.then_inc(ready[bank], 1)
                pe.sem_inc(xs_read, J)
            pe.wait_ge(sel_ready, 1)
            for b in range(2):
                pe.wait_ge(free[b], 1 + NT // J)
            pe.matmul(R[:, 0, 0:NT * E], upper[:, :], sel[:, :, :].rearrange("p t e -> p (t e)"), start=True, stop=True)
            pe.matmul(R[:, 1, 0:NT * E], ones[:, :], sel[:, :, :].rearrange("p t e -> p (t e)"),
                      start=True, stop=True).then_inc(sums_ready, 1)

        @block.vector
        def _(dve):
            ch = Chain(dve, c_dve)
            for n in range(NB):
                dve.sem_inc(free[n], 1)
            dve.sem_inc(xs_read, J)
            dve.wait_ge(w_in, 32)
            dve.wait_ge(consts, 1)
            if gate_bias is None:
                ch.link(dve.memset(gb[:, :], 0.0))
            with dve.Fori(0, NT // J) as i:
                for what, j, bank, value in looped(PLAN, i, NB, USES).steps():
                    if what == "g":
                        dve.wait_ge(ready[bank], value)
                        dve.tensor_tensor(sg[:, ds(J * i + j, 1), :].rearrange("p o e -> p (o e)"), R[:, bank, 0:E],
                                          gb[:, :], ALU.add).then_inc(free[bank], 1)
            for n in range(J):
                dve.wait_ge(free[J + n], 1 + NT // J)
            dve.sem_inc(logits, NT)
            dve.wait_ge(exp_done, 1)
            ch.link(dve.tensor_scalar(hot[:, :, :], hot[:, :, :], 1.0, None, ALU.add))
            ch.link(dve.reciprocal(sg[:, :, :], hot[:, :, :]))

            def ranks(to, v, N, W):
                mine, other = bcast(v, 3, W), bcast(v, 2, W)
                ca = cmp_a[:, 0:N * W * W].rearrange("p (n e j) -> p n e j", e=W, j=W)
                cb = cmp_b[:, 0:N * W * W].rearrange("p (n e j) -> p n e j", e=W, j=W)
                ch.done(dve.tensor_tensor(ca, other, mine, ALU.is_gt))
                ch.link(dve.tensor_tensor(cb, other, mine, ALU.is_equal))
                ch.link(dve.tensor_tensor(cb, cb, bcast(low[:, 0:W, 0:W], 1, N), ALU.mult))
                ch.link(dve.tensor_tensor(ca, ca, cb, ALU.add))
                ch.link(dve.tensor_reduce(to, ca, AX_X, ALU.add))

            choice = sg
            if E > 8:
                by_group = lambda m: m[:, :, :].rearrange("p t (g e) -> p (t g) e", e=GR)
                flat = lambda m: m[:, :, :].rearrange("p t g -> p (t g)")
                ranks(by_group(rank), by_group(sg), NT * E // GR, GR)
                ch.link(dve.tensor_scalar(hot[:, :, :], rank[:, :, :], 2.0, None, ALU.is_lt))
                ch.link(dve.tensor_tensor(hot[:, :, :], hot[:, :, :], sg[:, :, :], ALU.mult))
                ch.link(dve.tensor_reduce(flat(grp), by_group(hot), AX_X, ALU.add))
                ranks(grank[:, :, :], grp[:, :, :], NT, GR)
                ch.link(dve.tensor_scalar(grank[:, :, :], grank[:, :, :], 2.0, None, ALU.is_lt))
                allowed = bcast(flat(grank), 2, GR)
                ch.link(dve.tensor_tensor(by_group(ma), by_group(sg), allowed, ALU.mult))
                ch.link(dve.tensor_tensor(by_group(ma), by_group(ma), allowed, ALU.add))
                choice = ma
            ranks(rank[:, :, :], choice[:, :, :], NT, E)
            dve.tensor_scalar(sel[:, :, :], rank[:, :, :], float(K), None, ALU.is_lt).then_inc(sel_ready, 1)
            for r in range(K):
                ch.link(dve.tensor_scalar(hot[:, :, :], rank[:, :, :], float(r), None, ALU.is_equal))
                ch.link(dve.tensor_tensor(hot[:, :, :], hot[:, :, :], sg[:, :, :], ALU.mult))
                ch.link(dve.tensor_reduce(wgt[:, :, r], hot[:, :, :], AX_X, ALU.add))
            ch.link(dve.tensor_reduce(tot[:, :], wgt[:, :, :], AX_X, ALU.add))
            ch.link(dve.tensor_scalar(tot[:, :], tot[:, :], 1e-6, None, ALU.add))
            ch.link(dve.reciprocal(tot[:, :], tot[:, :]))
            ch.link(dve.tensor_tensor(wgt[:, :, :], wgt[:, :, :], bcast(tot[:, :], 2, K), ALU.mult))
            dve.wait_ge(sums_ready, 1)
            before = R[:, 0, 0:NT * E].rearrange("p (t e) -> p t e", e=E)
            total = R[:, 1, 0:NT * E].rearrange("p (t e) -> p t e", e=E)
            for e in range(E):
                ch.done(dve.tensor_tensor_scan(incl[:, :, e], one_f[:, :], total[:, :, e], 0.0, ALU.mult, ALU.add))
            ch.wait()
            ch.link(dve.tensor_tensor(place[:, :, :], incl[:, :, :], total, ALU.subtract))
            ch.link(dve.tensor_tensor(place[:, :, :], place[:, :, :], before, ALU.add))
            ch.link(dve.tensor_tensor(over[:, :, :], bcast(incl[:, NT - 1, :], 2, NT), bcast(steps[:, :], 1, E),
                                      ALU.is_gt))
            ch.link(dve.tensor_reduce(tiles[:, :], over[:, :, :], AX_X, ALU.add))
            ch.link(dve.tensor_tensor_scan(ends[:, :], one_f[:, 0:E], tiles[:, :], 0.0, ALU.mult, ALU.add))
            ch.link(dve.tensor_tensor(starts[:, :], ends[:, :], tiles[:, :], ALU.subtract))
            ch.link(dve.tensor_scalar(starts[:, :], starts[:, :], float(P), float(P * M.FIRST), ALU.mult, ALU.add))
            ch.link(dve.tensor_tensor(place[:, :, :], place[:, :, :], bcast(starts[:, :], 1, NT), ALU.add))
            for r in range(K):
                ch.link(dve.tensor_scalar(hot[:, :, :], rank[:, :, :], float(r), None, ALU.is_equal))
                ch.link(dve.tensor_tensor(hot[:, :, :], hot[:, :, :], place[:, :, :], ALU.mult))
                ch.link(dve.tensor_reduce(posf[:, :, r], hot[:, :, :], AX_X, ALU.add))
            ch.done(dve.tensor_copy(pos[:, :, :], posf[:, :, :]))
            ch.link(dve.tensor_tensor(past[:, :, :], bcast(item[:, :], 2, E), bcast(ends[0:1, :], 1, M.ROUTED),
                                      ALU.is_ge))
            ch.link(dve.tensor_reduce(idf[:, M.FIRST:M.FIRST + M.ROUTED], past[:, :, :], AX_X, ALU.add))
            ch.done(dve.tensor_scalar(idf[:, M.FIRST:M.FIRST + M.ROUTED], idf[:, M.FIRST:M.FIRST + M.ROUTED],
                                      float(E - 1), None, ALU.min))
            ch.done(dve.memset(idf[:, 0:M.FIRST], float(M.IDS[0])))
            ch.link(dve.memset(idf[:, M.FIRST + M.ROUTED:M.ITEMS], float(M.IDS[-1])))
            ch.link(dve.tensor_copy(ids[:, :], idf[:, :]))
    sc.close(G.spent)


def moe0_stage(nc, a, G, W):
    M = MIX0
    E, K, F = M.E, M.K, 1024
    FB = F // P
    keep = Scope(nc, "f0k")
    pos = keep.sb("pos", [P, NT, K], I32)
    wgt = keep.sb("wgt", [P, NT, K])
    ids = keep.sb("ids", [1, M.ITEMS], I32)
    Xd, Yd = a["Xd0"], a["Yd0"]
    routing_stage(nc, a, G, M, a["gate0"], a["gate_b0"], Xd, pos, wgt, ids, G.prefetch_down)

    sc = Scope(nc, "f0")
    sb, ps, sem = sc.sb, sc.ps, sc.sem
    NX = 4
    ub = sb("ub", [P, E + 1, FB])
    db = sb("db", [P, E + 1, D])
    xin = sb("xin", [P, NX, D])
    xT = sb("xT", [P, 2, KD, P])
    h = sb("h", [P, F])
    hT = sb("hT", [P, FB, P])
    yo = sb("yo", [P, 2, D])
    acc = sb("acc", [P, NT, D])
    ga = sb("ga", [P, 4, D])
    X = ps("X", [P, 512])
    U = ps("U", [P, 2, 512])
    TT = ps("TT", [P, 2, 512])
    Y = ps("Y", [P, 2, 512])
    b_in, scattered = sem("b_in"), sem("scattered")
    x_in = [sem(f"x_in{n}") for n in range(NX)]
    stored = [sem(f"stored{p}") for p in range(2)]
    gathered = [sem(f"gathered{p}") for p in range(2)]
    xt_ready, xt_done = sem("xt_ready"), sem("xt_done")
    up_ready, up_done = sem("up_ready"), sem("up_done")
    tr_ready, gelu_done = sem("tr_ready"), sem("gelu_done")
    dn_ready, dn_done = sem("dn_ready"), sem("dn_done")
    acc_done, c_pool = sem("acc_done"), sem("c_pool")
    N = M.ITEMS

    with nc.Block() as block:

        @block.sync
        def _(sp):
            sp.dma_start(ub[:, :, :], a["up_b"]).then_inc(b_in, 16)
            sp.dma_start(db[:, :, :], a["down_b"].partition_broadcast(P)).then_inc(b_in, 16)

            def load(u, n):
                sp.dma_start(xin[:, n, :], Xd[ds(u * P, P), :]).then_inc(x_in[n], 16)

            for u in range(NX):
                load(u, u)
            with sp.Fori(1, M.FIRST // NX) as q:
                for n in range(NX):
                    sp.wait_ge(xt_ready, NX * q + n + 1 - NX)
                    load(NX * q + n, n)
            sp.wait_ge(scattered, 16 * K * NT)
            with sp.Fori(M.FIRST // NX, N // NX) as q:
                for n in range(NX):
                    sp.wait_ge(xt_ready, NX * q + n + 1 - NX)
                    load(NX * q + n, n)

        def combine(pool, ch, t):
            g = 2 * (t % 2)
            pool.wait_ge(gathered[t % 2], 16 * K * (t // 2 + 1))
            ch.link(pool.tensor_scalar(acc[:, t, :], ga[:, g, :], wgt[:, t, 0:1], None, ALU.mult))
            ch.link(pool.tensor_scalar(ga[:, g + 1, :], ga[:, g + 1, :], wgt[:, t, 1:2], None, ALU.mult))
            ch.link(pool.tensor_tensor(acc[:, t, :], acc[:, t, :], ga[:, g + 1, :], ALU.add))

        @block.gpsimd
        def _(pool):
            ch = Chain(pool, c_pool, G.passed)
            pool.wait_ge(G.zeroed, 32)
            for t in range(NT):
                for r in range(K):
                    pool.indirect_dma_start(Xd[0:P * (M.FIRST + M.ROUTED), :], bass.IndirectOffsetOnAxis(pos[:, t, r:r + 1], 0),
                                            G.x_sb[:, t, :], None).then_inc(scattered, 16)
            for p in range(2):
                pool.wait_ge(stored[p], 16 * (M.FIRST + M.ROUTED) // 2)
            for t in range(NT):
                g = 2 * (t % 2)
                for r in range(K):
                    pool.indirect_dma_start(ga[:, g + r, :], None, Yd[0:P * (M.FIRST + M.ROUTED), :],
                                            bass.IndirectOffsetOnAxis(pos[:, t, r:r + 1], 0)).then_inc(gathered[t % 2], 16)
                if t:
                    combine(pool, ch, t - 1)
            combine(pool, ch, NT - 1)

        @block.scalar
        def _(act):
            def step(u, p, first=False):
                e = act.value_load(ids[0:1, ds(u, 1)], min_val=0, max_val=E)
                if not first:
                    act.wait_ge(dn_done, u)
                    act.dma_start(Yd[ds((u - 1) * P, P), :], yo[:, 1 - p, :]).then_inc(stored[1 - p], 16)
                for m in range(FB):
                    if m % 4 == 0:
                        act.wait_ge(tr_ready, 2 * u + m // 4 + 1)
                    if m == 0 and not first:
                        act.wait_ge(dn_ready, u)
                    g = act.activation(hT[:, m, :], TT[:, m // 4, (m % 4) * P:(m % 4 + 1) * P], ACT.Gelu,
                                       bias=ub[:, ds(e, 1), m])
                    if m % 4 == 3:
                        g.then_inc(gelu_done, 1)

            act.wait_ge(b_in, 32)
            step(0, 0, first=True)
            with act.Fori(0, (N - 2) // 2) as q:
                for n in range(2):
                    step(2 * q + n + 1, 1 - n)
            step(N - 1, 1)
            act.wait_ge(dn_done, N)
            act.dma_start(Yd[(N - 1) * P:N * P, :], yo[:, 1, :]).then_inc(stored[1], 16)
            for p in range(2):
                act.wait_ge(stored[p], 16 * N // 2)

        @block.vector
        def _(dve):
            def take_x(u, p):
                dve.wait_ge(xt_ready, u + 1)
                dve.tensor_copy(xT[:, p, :, :], X[:, 0:D].rearrange("p (k c) -> p k c", k=KD)).then_inc(xt_done, 1)

            def take_up(u):
                for n in range(2):
                    dve.wait_ge(up_ready, 2 * u + n + 1)
                    dve.tensor_copy(h[:, 512 * n:512 * n + 512], U[:, n, :]).then_inc(up_done, 1)

            def take_down(u, p, early=False):
                e = dve.value_load(ids[0:1, ds(u, 1)], min_val=0, max_val=E)
                dve.wait_ge(dn_ready, u + 1)
                if not early:
                    dve.wait_ge(stored[p], 16 * ((u - p) // 2))
                dve.tensor_tensor(yo[:, p, :], Y[:, p, 0:D], db[:, ds(e, 1), :].rearrange("p o c -> p (o c)"),
                                  ALU.add).then_inc(dn_done, 1)

            dve.wait_ge(b_in, 32)
            take_x(0, 0)
            take_up(0)
            take_x(1, 1)
            take_up(1)
            take_down(0, 0, early=True)
            take_x(2, 0)
            take_up(2)
            take_down(1, 1, early=True)
            take_x(3, 1)
            with dve.Fori(1, (N - 2) // 2) as q:
                for n in range(2):
                    u = 2 * q + n + 1
                    take_up(u)
                    take_down(u - 1, n)
                    take_x(u + 1, n)
            take_up(N - 1)
            take_down(N - 2, 0)
            take_down(N - 1, 1)

        @block.tensor
        def _(pe):
            def turn_x(u, n, early=False):
                pe.wait_ge(x_in[n], 16 * ((u - n) // NX) + 16)
                if not early:
                    pe.wait_ge(xt_done, u)
                for kk in range(KD):
                    mm = pe.transpose(X[:, kk * P:(kk + 1) * P], xin[:, n, kk * P:(kk + 1) * P], G.ident_f[:, :])
                mm.then_inc(xt_ready, 1)

            def up(u, p, first=False):
                e = pe.value_load(ids[0:1, ds(u, 1)], min_val=0, max_val=E)
                pe.wait_ge(xt_done, u + 1)
                for n in range(2):
                    if not first:
                        pe.wait_ge(up_done, 2 * u + n - 1)
                    for kk in range(KD):
                        mm = pe.matmul(U[:, n, :], xT[:, p, kk, :],
                                       W.up[:, ds(e, 1), kk, 512 * n:512 * n + 512].rearrange("p o c -> p (o c)"),
                                       start=(kk == 0), stop=(kk == KD - 1))
                    mm.then_inc(up_ready, 1)

            def turn_h(u, first=False):
                for n in range(2):
                    pe.wait_ge(up_done, 2 * u + n + 1)
                    if not first:
                        pe.wait_ge(gelu_done, 2 * u + n - 1)
                    for m in range(4):
                        mm = pe.transpose(TT[:, n, m * P:(m + 1) * P], h[:, 512 * n + m * P:512 * n + (m + 1) * P],
                                          G.ident_f[:, :])
                    mm.then_inc(tr_ready, 1)

            def down(u, p, early=False):
                e = pe.value_load(ids[0:1, ds(u, 1)], min_val=0, max_val=E)
                pe.wait_ge(gelu_done, 2 * u + 2)
                if not early:
                    pe.wait_ge(dn_done, u - 1)
                for m in range(FB):
                    mm = pe.matmul(Y[:, p, 0:D], hT[:, m, :], W.down[:, ds(e, 1), m, :].rearrange("p o c -> p (o c)"),
                                   start=(m == 0), stop=(m == FB - 1))
                mm.then_inc(dn_ready, 1)

            pe.wait_ge(G.up_in, G.UP_LOADS)
            pe.wait_ge(G.down_in, G.DOWN_LOADS)
            turn_x(0, 0, early=True)
            up(0, 0, first=True)
            turn_h(0, first=True)
            turn_x(1, 1)
            up(1, 1)
            down(0, 0, early=True)
            turn_h(1)
            turn_x(2, 2)
            up(2, 0)
            down(1, 1, early=True)
            turn_h(2)
            turn_x(3, 3)
            with pe.Fori(0, (N - NX) // NX) as q:
                for n in range(NX):
                    u = NX * q + n + NX - 1
                    up(u, 1 - n % 2)
                    down(u - 1, n % 2)
                    turn_h(u)
                    turn_x(u + 1, n)
            up(N - 1, 1)
            down(N - 2, 0)
            turn_h(N - 1)
            down(N - 1, 1)
    fin = Scope(nc, "f0f")
    finish_moe(nc, G, fin, M, Yd, acc, xin, scaled=True)
    fin.close(G.spent)
    sc.close(G.spent)
    keep.close(G.spent)


def finish_moe(nc, G, fin, M, Yd, acc, sh, scaled):
    sem = fin.sem
    J = 4
    SH = len(M.SHARED) // NT
    st = fin.sb("st", [P, J, 6])
    mv = fin.sb("mv", [P, J, 2])
    rstd = fin.sb("rstd", [P, J])
    half = fin.sb("half", [P, J])
    top = fin.sb("top", [P, J])
    y_in = [sem(f"y_in{n}") for n in range(4)]
    var_ready, rstd_ready, c_dve, c_pool, done = [sem(n) for n in ("var_ready", "rstd_ready", "c_dve", "c_pool", "done")]
    with nc.Block() as block:

        @block.sync
        def _(sp):
            for s in range(SH):
                for t in range(NT):
                    n = s * NT + t
                    if n >= 4:
                        sp.wait_ge(done, n - 3)
                    sp.dma_start(sh[:, n % 4, :], Yd[M.row_of_shared(n):M.row_of_shared(n) + P, :]).then_inc(y_in[n % 4], 16)

        @block.gpsimd
        def _(pool):
            ch = Chain(pool, c_pool, G.passed)
            ch.link(pool.memset(half[:, :], -0.5))
            for i in range(NT // J):
                pool.wait_ge(var_ready, i + 1)
                ch.link(pool.tensor_scalar(rstd[:, :], mv[:, :, 1], LN_EPS, None, ALU.add))
                pool.tensor_tensor(rstd[:, :], rstd[:, :], half[:, :], ALU.pow).then_inc(rstd_ready, 1)

        @block.vector
        def _(dve):
            ch = Chain(dve, c_dve)
            for n in range(SH * NT):
                t = n % NT
                dve.wait_ge(y_in[n % 4], 16 * (n // 4) + 16)
                if n >= NT:
                    dve.wait_ge(done, n - NT + 1)
                dve.tensor_tensor(acc[:, t, :], acc[:, t, :], sh[:, n % 4, :], ALU.add).then_inc(done, 1)
                if n < (SH - 1) * NT or t % J < J - 1:
                    continue
                i = t // J
                tiles = range(J * i, J * i + J)
                dve.wait_ge(done, n + 1)
                if scaled:
                    ch.link(dve.tensor_reduce(top[:, :], acc[:, J * i:J * i + J, :], AX_X, ALU.max,
                                              apply_absolute_value=True))
                    ch.link(dve.tensor_scalar(top[:, :], top[:, :], 0.1, 1e-6, ALU.mult, ALU.add))
                    ch.link(dve.reciprocal(top[:, :], top[:, :]))
                    ch.link(dve.tensor_scalar(top[:, :], top[:, :], 0.1, None, ALU.mult))
                    for j, tt in enumerate(tiles):
                        ch.done(dve.scalar_tensor_tensor(acc[:, tt, :], acc[:, tt, :], top[:, j:j + 1],
                                                         G.x_sb[:, tt, :], ALU.mult, ALU.add))
                else:
                    ch.done(dve.tensor_tensor(acc[:, J * i:J * i + J, :], acc[:, J * i:J * i + J, :],
                                              G.x_sb[:, J * i:J * i + J, :], ALU.add))
                ch.wait()
                for j, tt in enumerate(tiles):
                    ch.done(dve.bn_stats(st[:, j, :], acc[:, tt, :]))
                ch.wait()
                for j in range(J):
                    last = dve.bn_aggr(mv[:, j, :], st[:, j, :])
                last.then_inc(var_ready, 1)
                dve.wait_ge(rstd_ready, i + 1)
                for j, tt in enumerate(tiles):
                    ch.done(dve.tensor_scalar(G.x_sb[:, tt, :], acc[:, tt, :], mv[:, j, 0:1], rstd[:, j:j + 1],
                                              ALU.subtract, ALU.mult))
                ch.wait()


def rwkv_stage(nc, a, G):
    sc = Scope(nc, "rk")
    sb, sem = sc.sb, sc.sem
    J, H = 4, 512
    S1 = S + 1
    w = sb("w", [P, 4, KD, D])
    cols = sb("cols", [P, 7, KD])
    decay = sb("decay", [P, KD])
    first = sb("first", [P, KD])
    half = sb("half", [P, J])
    xt = sb("xt", [P, KD, B * S1])
    w_in = sem("w_in")

    na = Scope(nc, "rn")
    xn = na.sb("xn", [P, 2, J, D])
    st = na.sb("st", [P, 2, J, 6])
    mv = na.sb("mv", [P, 2, J, 2])
    rstd = na.sb("rstd", [P, 2, J])
    TB_ = na.ps("T", [P, 4, 512])
    var_ready, rstd_ready, xn_ready = na.sem("var_ready"), na.sem("rstd_ready"), na.sem("xn_ready")
    t_ready, t_copied = na.sem("t_ready"), na.sem("t_copied")
    c_dve, c_pool = na.sem("c_dve"), na.sem("c_pool")
    with nc.Block() as block:

        @block.sync
        def _(sp):
            sp.dma_start(cols[:, :, :], a["rwkv_cols"]).then_inc(w_in, 16)
            sp.dma_start(w[:, :, :, :], a["rwkv_w"]).then_inc(w_in, 16)

        @block.gpsimd
        def _(pool):
            ch = Chain(pool, c_pool, G.passed)
            ch.link(pool.memset(half[:, :], -0.5))
            for b in range(B):
                pool.memset(xt[:, :, b * S1:b * S1 + 1], 0.0)
            with pool.Fori(0, B) as b:
                ch.enter(b, 2)
                for c in range(2):
                    pool.wait_ge(var_ready, 2 * b + c + 1)
                    settle(pool, G.passed)
                    ch.link(pool.tensor_scalar(rstd[:, c, :], mv[:, c, :, 1], LN_EPS, None, ALU.add))
                    pool.tensor_tensor(rstd[:, c, :], rstd[:, c, :], half[:, :], ALU.pow).then_inc(rstd_ready, 1)
                ch.leave(B)

        @block.scalar
        def _(act):
            act.wait_ge(w_in, 32)
            act.activation(decay[:, :], cols[:, 5, :], ACT.Sigmoid)
            act.activation(first[:, :], cols[:, 6, :], ACT.Exp)
            with act.Fori(0, B) as b:
                for c in range(2):
                    for kk in range(KD):
                        act.wait_ge(t_ready, 4 * b + 2 * c + kk + 2)
                        act.activation(xt[:, kk, ds(b * S1 + 1 + c * H, H)], TB_[:, 2 * c + kk, :], ACT.Identity,
                                       bias=cols[:, 1, kk:kk + 1], scale=cols[:, 0, kk:kk + 1]).then_inc(t_copied, 1)

        @block.vector
        def _(dve):
            ch = Chain(dve, c_dve)
            dve.sem_inc(t_copied, 4)
            dve.sem_inc(t_ready, 1)
            with dve.Fori(0, B) as b:
                ch.enter(b, 2 * J)
                x_of = lambda c, j: G.x_sb[:, ds(TB * b + J * c + j, 1), :].rearrange("p o c -> p (o c)")
                for c in range(2):
                    n = [ch.done(dve.bn_stats(st[:, c, j, :], x_of(c, j))) for j in range(J)]
                    for j in range(J):
                        ch.wait(n[j])
                        settle(dve, G.passed)
                        last = dve.bn_aggr(mv[:, c, j, :], st[:, c, j, :])
                    last.then_inc(var_ready, 1)
                for c in range(2):
                    dve.wait_ge(rstd_ready, 2 * b + c + 1)
                    dve.wait_ge(t_ready, 4 * b + 1)
                    for j in range(J):
                        dve.tensor_scalar(xn[:, c, j, :], x_of(c, j), mv[:, c, j, 0:1], rstd[:, c, j:j + 1],
                                          ALU.subtract, ALU.mult).then_inc(xn_ready, 1)
                ch.leave(B)

        @block.tensor
        def _(pe):
            with pe.Fori(0, B) as b:
                for c in range(2):
                    for kk in range(KD):
                        pe.wait_ge(t_copied, 4 * b + 2 * c + kk + 1)
                        for j in range(J):
                            pe.wait_ge(xn_ready, 2 * J * b + J * c + j + 1)
                            mm = pe.transpose(TB_[:, 2 * c + kk, j * P:(j + 1) * P], xn[:, c, j, kk * P:(kk + 1) * P],
                                              G.ident_f[:, :])
                        mm.then_inc(t_ready, 1)
    na.close(G.spent)

    mm_ = Scope(nc, "rm")
    sb, ps, sem = mm_.sb, mm_.ps, mm_.sem
    NB = 8
    diff = sb("diff", [P, 2, KD, H])
    xm = sb("xm", [P, 2, 3, KD, H])
    state = sb("state", [P, 2, KD, H])
    sig = sb("sig", [P, 2, KD, H])
    rw = sb("rw", [P, KD, S])
    xr = sb("xr", [P, J, D])
    st = sb("st", [P, J, 6])
    mv = sb("mv", [P, J, 2])
    rstd = sb("rstd", [P, J])
    R = ps("R", [P, NB, 512])
    ready = [sem(f"bank_ready{n}") for n in range(NB)]
    free = [sem(f"bank_free{n}") for n in range(NB)]
    diff_ready, scaled = sem("diff_ready"), sem("scaled")
    mix_ready, sig_ready, rw_ready = sem("mix_ready"), sem("sig_ready"), sem("rw_ready")
    var_ready, rstd_ready = sem("var_ready"), sem("rstd_ready")
    c_dve, c_pool = sem("c_dve"), sem("c_pool")
    CREDIT = 4
    PLAN = []
    for c in range(2):
        PLAN += [(n, 2 * c + d) for n in "kvr" for d in range(KD)]
    PLAN += [("y", t) for t in range(TB)]
    USES = ("k", "v", "r", "y")

    with nc.Block() as block:

        @block.gpsimd
        def _(pool):
            ch = Chain(pool, c_pool, G.passed)
            with pool.Fori(0, B) as b:
                ch.enter(b, 2)
                for c in range(2):
                    now, prev = [xt[:, :, ds(b * S1 + 1 - back + c * H, H)] for back in (0, 1)]
                    pool.tensor_tensor(diff[:, c, :, :], now, prev, ALU.subtract).then_inc(diff_ready, 1)
                    for n in range(3):
                        pool.wait_ge(scaled, 12 * b + 6 * c + KD * (n + 1))
                        settle(pool, G.passed)
                        pool.tensor_tensor(xm[:, c, n, :, :], xm[:, c, n, :, :], prev, ALU.add).then_inc(mix_ready, 1)
                for k in range(2):
                    pool.wait_ge(var_ready, 2 * b + k + 1)
                    settle(pool, G.passed)
                    ch.link(pool.tensor_scalar(rstd[:, :], mv[:, :, 1], LN_EPS, None, ALU.add))
                    pool.tensor_tensor(rstd[:, :], rstd[:, :], half[:, :], ALU.pow).then_inc(rstd_ready, 1)
                ch.leave(B)

        @block.scalar
        def _(act):
            with act.Fori(0, B) as b:
                for c in range(2):
                    act.wait_ge(diff_ready, 2 * b + c + 1)
                    act.wait_ge(rw_ready, 4 * b + 2 * c + 2)
                    for n in range(3):
                        for kk in range(KD):
                            act.activation(xm[:, c, n, kk, :], diff[:, c, kk, :], ACT.Copy,
                                           scale=cols[:, 2 + n, kk:kk + 1]).then_inc(scaled, 1)
                for what, k, bank, value in looped(PLAN, b, NB, USES).steps():
                    if what == "r":
                        act.wait_ge(ready[bank], value)
                        act.wait_ge(rw_ready, 4 * b + k + 1)
                        act.activation(sig[:, k // 2, k % 2, :], R[:, bank, :], ACT.Sigmoid).then_inc(free[bank], 1)

        @block.vector
        def _(dve):
            ch = Chain(dve, c_dve)
            for n in range(NB):
                dve.sem_inc(free[n], 1)
            dve.sem_inc(rw_ready, CREDIT)
            with dve.Fori(0, B) as b:
                ch.enter(b, 4 + 2 * TB)
                placed = looped(PLAN, b, NB, USES)
                x_of = lambda t: G.x_sb[:, ds(TB * b + t, 1), :].rearrange("p o c -> p (o c)")
                for c in range(2):
                    scans, sums, prods = [], [], []
                    for d in range(KD):
                        bank, value = placed.value(("k", 2 * c + d))
                        dve.wait_ge(ready[bank], value)
                        start = state[:, 0, d, H - 1:H] if c else 0.0
                        scans.append(ch.done(dve.tensor_tensor_scan(
                            state[:, c, d, :], decay[:, d:d + 1].to_broadcast([P, H]), R[:, bank, :], start,
                            ALU.mult, ALU.add)))
                    for d in range(KD):
                        bank, value = placed.value(("k", 2 * c + d))
                        ch.wait(scans[d])
                        to = rw[:, d, c * H:(c + 1) * H]
                        sums.append(value)
                        dve.scalar_tensor_tensor(to, state[:, c, d, :], first[:, d:d + 1], R[:, bank, :],
                                                 ALU.mult, ALU.add).then_inc(free[bank], 1)
                    for d in range(KD):
                        kb, kv = placed.value(("k", 2 * c + d))
                        bank, value = placed.value(("v", 2 * c + d))
                        dve.wait_ge(ready[bank], value)
                        dve.wait_ge(free[kb], kv + 1)
                        to = rw[:, d, c * H:(c + 1) * H]
                        dve.tensor_tensor(to, to, R[:, bank, :], ALU.mult).then_inc(free[bank], 1)
                    for d in range(KD):
                        vb, vv = placed.value(("v", 2 * c + d))
                        bank, value = placed.value(("r", 2 * c + d))
                        dve.wait_ge(free[bank], value + 1)
                        dve.wait_ge(free[vb], vv + 1)
                        to = rw[:, d, c * H:(c + 1) * H]
                        dve.tensor_tensor(to, to, sig[:, c, d, :], ALU.mult).then_inc(rw_ready, 1)
                for k in range(2):
                    for j in range(J):
                        bank, value = placed.value(("y", J * k + j))
                        dve.wait_ge(ready[bank], value)
                        dve.scalar_tensor_tensor(xr[:, j, :], x_of(J * k + j), 2.0, R[:, bank, 0:D], ALU.mult,
                                                 ALU.add).then_inc(free[bank], 1)
                    n = []
                    for j in range(J):
                        bank, value = placed.value(("y", J * k + j))
                        dve.wait_ge(free[bank], value + 1)
                        n.append(ch.done(dve.bn_stats(st[:, j, :], xr[:, j, :])))
                    for j in range(J):
                        ch.wait(n[j])
                        settle(dve, G.passed)
                        last = dve.bn_aggr(mv[:, j, :], st[:, j, :])
                    last.then_inc(var_ready, 1)
                    dve.wait_ge(rstd_ready, 2 * b + k + 1)
                    for j in range(J):
                        ch.done(dve.tensor_scalar(x_of(J * k + j), xr[:, j, :], mv[:, j, 0:1], rstd[:, j:j + 1],
                                                  ALU.subtract, ALU.mult))
                    ch.wait()
                ch.leave(B)

        @block.tensor
        def _(pe):
            with pe.Fori(0, B) as b:
                for what, k, bank, value in looped(PLAN, b, NB, USES).steps():
                    pe.wait_ge(free[bank], value)
                    if what == "y":
                        pe.wait_ge(rw_ready, 4 * b + CREDIT + 2 * (k // J) + 2)
                        for d in range(KD):
                            mm = pe.matmul(R[:, bank, 0:D], rw[:, d, k * P:(k + 1) * P], w[:, 3, d, :],
                                           start=(d == 0), stop=(d == KD - 1))
                    else:
                        c, d, n = k // 2, k % 2, "kvr".index(what)
                        pe.wait_ge(mix_ready, 6 * b + 3 * c + n + 1)
                        for kk in range(KD):
                            mm = pe.matmul(R[:, bank, :], w[:, n, kk, d * P:(d + 1) * P], xm[:, c, n, kk, :],
                                           start=(kk == 0), stop=(kk == KD - 1))
                    mm.then_inc(ready[bank], 1)
    mm_.close(G.spent)
    sc.close(G.spent)


def xattn1_stage(nc, a, G):
    sc = Scope(nc, "xb")
    sb, ps, sem = sc.sb, sc.ps, sc.sem
    J = 4
    SK = 64
    K2 = B * SK
    wq = sb("wq", [P, KD, D])
    wkT = sb("wkT", [P, KD, D])
    ctxT = sb("ctxT", [P, KD, K2])
    ctx = sb("ctx", [SK, B, D])
    bq = sb("bq", [P, KD])
    bk = sb("bk", [P, KD])
    m_i = sb("m_i", [P, K2], I32)
    m_f = sb("m_f", [P, K2])
    scale = sb("scale", [P, K2])
    hide = sb("hide", [1, K2])
    row = sb("row", [1, K2])
    one = sb("one", [1, P])
    kT = sb("kT", [P, KD, K2])
    km = sb("km", [P, KD, K2])
    half = sb("half", [P, J])
    xs = sb("xs", [P, 2, J, D])
    xT = sb("xT", [P, 2, J, KD, P])
    top = sb("top", [P, 2, J])
    sub = sb("sub", [P, 2, J, SK])
    e = sb("e", [P, 2, J, SK])
    den = sb("den", [P, 2, J])
    rden = sb("rden", [P, 2, J])
    aT = sb("aT", [SK, 2, J * P])
    xr = sb("xr", [P, J, D])
    st = sb("st", [P, J, 6])
    mv = sb("mv", [P, J, 2])
    rstd = sb("rstd", [P, J])
    TX = ps("TX", [P, 2, 512])
    SC = ps("SC", [P, 2, 512])
    TA = ps("TA", [P, 2, 512])
    O = ps("O", [P, 2, 512])
    w_in, set_up, kt_ready, kt_done = sem("w_in"), sem("set_up"), sem("kt_ready"), sem("kt_done")
    km_ready, km_done = sem("km_ready"), sem("km_done")
    xs_ready, tx_ready, tx_copied = sem("xs_ready"), sem("tx_ready"), sem("tx_copied")
    s_ready, s_read, exp_done = sem("s_ready"), sem("s_read"), sem("exp_done")
    a_ready, a_copied, o_ready, o_read = sem("a_ready"), sem("a_copied"), sem("o_ready"), sem("o_read")
    var_ready, rstd_ready, c_dve, c_pool = sem("var_ready"), sem("rstd_ready"), sem("c_dve"), sem("c_pool")
    CU, CN = 2, 4
    NU_ = NT // J
    LOADS = 7

    with nc.Block() as block:

        @block.sync
        def _(sp):
            for to, name in ((wkT, "xk1"), (ctxT, "ctxT"), (wq, "xq1")):
                sp.dma_start(to[:, :, :], a[name]).then_inc(w_in, 16)
            sp.dma_start(bk[:, :], a["bk1"]).then_inc(w_in, 16)
            sp.dma_start(bq[:, :], a["bq1"]).then_inc(w_in, 16)
            sp.dma_start(m_i[:, :], a["mask1"].rearrange("b k -> (b k)").partition_broadcast(P)).then_inc(w_in, 16)
            sp.dma_start(ctx[:, :, :], a["ctx"]).then_inc(w_in, 16)

        @block.gpsimd
        def _(pool):
            ch = Chain(pool, c_pool, G.passed)
            pool.memset(one[:, :], 1.0)
            ch.link(pool.memset(half[:, :], -0.5))
            pool.wait_ge(w_in, 16 * LOADS)
            ch.link(pool.tensor_copy(m_f[:, :], m_i[:, :]))
            pool.tensor_scalar(scale[:, :], m_f[:, :], float(D) ** -0.5, None, ALU.mult)
            pool.tensor_scalar(hide[:, :], m_f[0:1, :], 0.0, -1e9, ALU.is_equal, ALU.mult).then_inc(set_up, 1)
            with pool.Fori(0, NU_ // 2) as b:
                ch.enter(b, 2)
                for c in range(2):
                    u = 2 * b + c
                    pool.wait_ge(tx_copied, 2 * u + CN - 2)
                    for j in range(J):
                        pool.tensor_copy(xs[:, c, j, :], G.x_sb[:, ds(J * u + j, 1), :].rearrange("p o c -> p (o c)")
                                         ).then_inc(xs_ready, 1)
                for c in range(2):
                    pool.wait_ge(var_ready, 2 * b + c + 1)
                    settle(pool, G.passed)
                    ch.link(pool.tensor_scalar(rstd[:, :], mv[:, :, 1], LN_EPS, None, ALU.add))
                    pool.tensor_tensor(rstd[:, :], rstd[:, :], half[:, :], ALU.pow).then_inc(rstd_ready, 1)
                ch.leave(NU_ // 2)

        @block.scalar
        def _(act):
            act.wait_ge(w_in, 16 * LOADS)
            for d in range(KD):
                act.wait_ge(kt_ready, d + 1)
                act.activation(kT[:, d, :], TX[:, d, 0:K2], ACT.Identity, bias=bk[:, d:d + 1]).then_inc(kt_done, 1)
            with act.Fori(0, NU_ // 2) as b:
                for c in range(2):
                    u = 2 * b + c
                    act.wait_ge(s_ready, u + CU - 1)
                    for n in range(2):
                        act.wait_ge(tx_ready, 2 * u + n + 1)
                        act.activation(xT[:, c, 2 * n:2 * n + 2, :, :],
                                       TX[:, n, :].rearrange("p (t k q) -> p t k q", t=2, k=KD), ACT.Copy
                                       ).then_inc(tx_copied, 1)
                for c in range(2):
                    u = 2 * b + c
                    act.wait_ge(s_read, u + CU + 1)
                    act.wait_ge(a_ready, u + CU - 1)
                    act.activation(e[:, c, :, :], sub[:, c, :, :], ACT.Exp).then_inc(exp_done, 1)
                for c in range(2):
                    u = 2 * b + c
                    act.wait_ge(a_ready, u + CU + 1)
                    act.wait_ge(o_ready, 2 * u + CN - 2)
                    act.activation(aT[:, c, :], TA[0:SK, c, :], ACT.Copy).then_inc(a_copied, 1)

        @block.vector
        def _(dve):
            ch = Chain(dve, c_dve)
            for s, n in ((tx_copied, CN), (s_ready, CU), (s_read, CU), (exp_done, CU), (a_ready, CU), (a_copied, CU),
                         (o_ready, CN), (o_read, CN)):
                dve.sem_inc(s, n)
            dve.wait_ge(set_up, 1)
            for d in range(KD):
                dve.wait_ge(km_ready, d + 1)
                dve.tensor_tensor(km[:, d, :], SC[:, d, 0:K2], scale[:, :], ALU.mult).then_inc(km_done, 1)
            dve.wait_ge(km_ready, KD + 1)
            ch.link(dve.tensor_tensor(row[:, :], TA[0:1, 0, 0:K2], scale[0:1, :], ALU.mult))
            dve.tensor_tensor(row[:, :], row[:, :], hide[:, :], ALU.add).then_inc(km_done, 1)
            with dve.Fori(0, NU_ // 2) as b:
                ch.enter(b, 2 * (3 + 2 * J))
                x_of = lambda t: G.x_sb[:, ds(t, 1), :].rearrange("p o c -> p (o c)")
                for c in range(2):
                    u = 2 * b + c
                    dve.wait_ge(s_ready, u + CU + 1)
                    scores = SC[:, c, 0:J * SK].rearrange("p (t k) -> p t k", k=SK)
                    ch.link(dve.tensor_reduce(top[:, c, :], scores, AX_X, ALU.max))
                    dve.wait_ge(exp_done, u + CU - 1)
                    dve.tensor_tensor(sub[:, c, :, :], scores, bcast(top[:, c, :], 2, SK), ALU.subtract
                                      ).then_inc(s_read, 1)
                for c in range(2):
                    dve.wait_ge(exp_done, 2 * b + c + CU + 1)
                    ch.link(dve.tensor_reduce(den[:, c, :], e[:, c, :, :], AX_X, ALU.add))
                    ch.link(dve.reciprocal(rden[:, c, :], den[:, c, :]))
                for c in range(2):
                    u = 2 * b + c
                    for j in range(J):
                        if j % 2 == 0:
                            dve.wait_ge(o_ready, 2 * u + j // 2 + CN + 1)
                        n = dve.scalar_tensor_tensor(xr[:, j, :], O[:, j // 2, D * (j % 2):D * (j % 2) + D],
                                                     rden[:, c, j:j + 1], x_of(J * u + j), ALU.mult, ALU.add)
                        if j % 2:
                            n.then_inc(o_read, 1)
                    dve.wait_ge(o_read, 2 * u + CN + 2)
                    n = [ch.done(dve.bn_stats(st[:, j, :], xr[:, j, :])) for j in range(J)]
                    for j in range(J):
                        ch.wait(n[j])
                        settle(dve, G.passed)
                        last = dve.bn_aggr(mv[:, j, :], st[:, j, :])
                    last.then_inc(var_ready, 1)
                    dve.wait_ge(rstd_ready, u + 1)
                    for j in range(J):
                        ch.done(dve.tensor_scalar(x_of(J * u + j), xr[:, j, :], mv[:, j, 0:1], rstd[:, j:j + 1],
                                                  ALU.subtract, ALU.mult))
                    ch.wait()
                ch.leave(NU_ // 2)

        @block.tensor
        def _(pe):
            pe.wait_ge(w_in, 16 * LOADS)
            for d in range(KD):
                for kk in range(KD):
                    mm = pe.matmul(TX[:, d, 0:K2], wkT[:, kk, d * P:(d + 1) * P], ctxT[:, kk, :],
                                   start=(kk == 0), stop=(kk == KD - 1))
                mm.then_inc(kt_ready, 1)
            pe.wait_ge(kt_done, KD)
            for d in range(KD):
                for kk in range(KD):
                    mm = pe.matmul(SC[:, d, 0:K2], wq[:, kk, d * P:(d + 1) * P], kT[:, kk, :],
                                   start=(kk == 0), stop=(kk == KD - 1))
                mm.then_inc(km_ready, 1)
            for kk in range(KD):
                mm = pe.matmul(TA[0:1, 0, 0:K2], bq[:, kk:kk + 1], kT[:, kk, :], start=(kk == 0), stop=(kk == KD - 1))
            mm.then_inc(km_ready, 1)
            pe.wait_ge(km_done, KD + 1)
            with pe.Fori(0, NU_ // 2) as b:
                for c in range(2):
                    u = 2 * b + c
                    for n in range(2):
                        pe.wait_ge(tx_copied, 2 * u + n + CN - 1)
                        for t in range(2):
                            pe.wait_ge(xs_ready, J * u + 2 * n + t + 1)
                            for kk in range(KD):
                                mm = pe.transpose(TX[:, n, (KD * t + kk) * P:(KD * t + kk + 1) * P],
                                                  xs[:, c, 2 * n + t, kk * P:(kk + 1) * P], G.ident_f[:, :])
                        mm.then_inc(tx_ready, 1)
                    pe.wait_ge(s_read, u + CU - 1)
                    for j in range(J):
                        if j % 2 == 0:
                            pe.wait_ge(tx_copied, 2 * u + j // 2 + CN + 1)
                        to = SC[:, c, j * SK:(j + 1) * SK]
                        for kk in range(KD):
                            pe.matmul(to, xT[:, c, j, kk, :], km[:, kk, ds(b * SK, SK)], start=(kk == 0), stop=False)
                        mm = pe.matmul(to, one[:, :], row[:, ds(b * SK, SK)], start=False, stop=True)
                    mm.then_inc(s_ready, 1)
                for c in range(2):
                    u = 2 * b + c
                    pe.wait_ge(exp_done, u + CU + 1)
                    pe.wait_ge(a_copied, u + CU - 1)
                    settle(pe, G.passed)
                    for j in range(J):
                        mm = pe.transpose(TA[0:SK, c, j * P:(j + 1) * P], e[:, c, j, :], G.ident_f[:, :])
                    mm.then_inc(a_ready, 1)
                    pe.wait_ge(a_copied, u + CU + 1)
                    settle(pe, G.passed)
                    for n in range(2):
                        pe.wait_ge(o_read, 2 * u + n + CN - 1)
                        settle(pe, G.passed)
                        for t in range(2):
                            j = 2 * n + t
                            mm = pe.matmul(O[:, n, t * D:(t + 1) * D], aT[:, c, j * P:(j + 1) * P],
                                           ctx[:, ds(b, 1), :].rearrange("p o c -> p (o c)"), start=True, stop=True)
                        mm.then_inc(o_ready, 1)
    sc.close(G.spent)


def moe1_stage(nc, a, G):
    M = MIX1
    E, K, F = M.E, M.K, P
    EX = E + 2
    ws = Scope(nc, "w1")
    w13 = ws.sb("w13", [P, EX, KD, 2 * F])
    w2 = ws.sb("w2", [P, EX, D])
    pos = ws.sb("pos", [P, NT, K], I32)
    wgt = ws.sb("wgt", [P, NT, K])
    ids = ws.sb("ids", [1, M.ITEMS], I32)
    weights_in = ws.sem("weights_in")
    Xd, Yd = a["Xd1"], a["Yd1"]

    def load_weights(sp):
        for e in range(0, EX, 3):
            sp.dma_start(w13[:, e:e + 3, :, :], a["w13"][:, e:e + 3, :, :]).then_inc(weights_in, 16)
        sp.dma_start(w2[:, :, :], a["w2"]).then_inc(weights_in, 16)

    WEIGHT_LOADS = EX // 3 + 1
    routing_stage(nc, a, G, M, a["gate1"], None, Xd, pos, wgt, ids, load_weights)

    sc = Scope(nc, "f1")
    sb, ps, sem = sc.sb, sc.ps, sc.sem
    NX, J = 4, 4
    N = M.ITEMS // 2
    FIRST, ROUTED = M.FIRST // 2, M.ROUTED // 2
    assert N % NX == 0 and FIRST % NX == 0
    xin = sb("xin", [P, NX, 2, D])
    xT = sb("xT", [P, 2, 2, KD, P])
    g = sb("g", [P, 2, 2, F])
    h = sb("h", [P, 2, 2, F])
    hT = sb("hT", [P, 2, 2, P])
    yo = sb("yo", [P, 2, 2, D])
    ga = sb("ga", [P, NT, K, D])
    sh = sb("sh", [P, 2, NT, D])
    st = sb("st", [P, J, 6])
    mv = sb("mv", [P, J, 2])
    rstd = sb("rstd", [P, J])
    half = sb("half", [P, J])
    X = ps("X", [P, 2, 512])
    U = ps("U", [P, 2, 512])
    TT = ps("TT", [P, 2, 512])
    Y = ps("Y", [P, 2, 512])
    scattered = sem("scattered")
    x_in = [sem(f"x_in{n}") for n in range(NX)]
    stored = [sem(f"stored{p}") for p in range(2)]
    gathered = [sem(f"gathered{t}") for t in range(NT)]
    sh_in = [sem(f"sh_in{s}") for s in range(2)]
    xt_ready, xt_done = sem("xt_ready"), sem("xt_done")
    up_ready, silu_done, h_done = sem("up_ready"), sem("silu_done"), sem("h_done")
    tr_ready, ht_done = sem("tr_ready"), sem("ht_done")
    dn_ready, y_done = sem("dn_ready"), sem("y_done")
    var_ready, rstd_ready, c_dve, c_pool = sem("var_ready"), sem("rstd_ready"), sem("c_dve"), sem("c_pool")
    CREDIT = 2

    def pipelined(eng, first, body, last):
        first()
        for q in (1, 2):
            body(q, q % NX)
        with eng.Fori(0, (N - NX) // NX) as r:
            for n in range(NX):
                body(NX * r + NX - 1 + n, (NX - 1 + n) % NX)
        last()

    with nc.Block() as block:

        @block.sync
        def _(sp):
            def load(q, n):
                sp.dma_start(xin[:, n, :, :], Xd[ds(q * 2 * P, 2 * P), :].rearrange("(i p) c -> p i c", p=P)
                             ).then_inc(x_in[n], 16)

            for q in range(NX):
                load(q, q)
            for q0, q1 in ((1, FIRST // NX), (FIRST // NX, N // NX)):
                if q0 > 1:
                    sp.wait_ge(scattered, 16 * K * NT)
                with sp.Fori(q0, q1) as r:
                    for n in range(NX):
                        sp.wait_ge(xt_ready, NX * r + n + 1 - NX)
                        load(NX * r + n, n)
            for s, pairs in ((0, FIRST), (1, N)):
                row = M.row_of_shared(s * NT)
                for p in range(2):
                    sp.wait_ge(stored[p], 16 + 16 * pairs // 2)
                sp.dma_start(sh[:, s, :, :], Yd[row:row + P * NT, :].rearrange("(t p) c -> p t c", p=P)
                             ).then_inc(sh_in[s], 16)

        @block.gpsimd
        def _(pool):
            ch = Chain(pool, c_pool, G.passed)
            ch.link(pool.memset(half[:, :], -0.5))
            pool.wait_ge(G.zeroed, 32)
            for t in range(NT):
                for r in range(K):
                    pool.indirect_dma_start(Xd[0:P * (M.FIRST + M.ROUTED), :],
                                            bass.IndirectOffsetOnAxis(pos[:, t, r:r + 1], 0),
                                            G.x_sb[:, t, :], None).then_inc(scattered, 16)
            for p in range(2):
                pool.wait_ge(stored[p], 16 + 16 * (FIRST + ROUTED) // 2)
            for t in range(NT):
                for r in range(K):
                    pool.indirect_dma_start(ga[:, t, r, :], None, Yd[0:P * (M.FIRST + M.ROUTED), :],
                                            bass.IndirectOffsetOnAxis(pos[:, t, r:r + 1], 0)).then_inc(gathered[t], 16)
            for i in range(NT // J):
                pool.wait_ge(var_ready, i + 1)
                ch.link(pool.tensor_scalar(rstd[:, :], mv[:, :, 1], LN_EPS, None, ALU.add))
                pool.tensor_tensor(rstd[:, :], rstd[:, :], half[:, :], ALU.pow).then_inc(rstd_ready, 1)

        @block.scalar
        def _(act):
            def silu(q, p):
                act.wait_ge(up_ready, q + 1 + CREDIT)
                act.wait_ge(h_done, q + 1)
                act.activation(g[:, p, :, :], U[:, p, :].rearrange("p (i f) -> p i f", i=2)[:, :, 0:F], ACT.Silu
                               ).then_inc(silu_done, 1)

            def result(q, p):
                act.wait_ge(dn_ready, q + 1 + CREDIT)
                act.wait_ge(stored[p], 16 * ((q - p) // 2) + 16)
                act.activation(yo[:, p, :, :], Y[:, p, :].rearrange("p (i c) -> p i c", i=2), ACT.Copy).then_inc(y_done, 1)
                act.wait_ge(y_done, q + 1 + CREDIT)
                act.dma_start(Yd[ds(q * 2 * P, 2 * P), :].rearrange("(i p) c -> p i c", p=P), yo[:, p, :, :]
                              ).then_inc(stored[p], 16)

            def body(q, n):
                silu(q, n % 2)
                result(q - 1, 1 - n % 2)

            def last():
                body(N - 1, 1)
                result(N - 1, 1)

            pipelined(act, lambda: silu(0, 0), body, last)
            for p in range(2):
                act.wait_ge(stored[p], 16 + 16 * N // 2)

        @block.vector
        def _(dve):
            ch = Chain(dve, c_dve)
            for s in (xt_done, up_ready, h_done, tr_ready, ht_done, dn_ready, y_done):
                dve.sem_inc(s, CREDIT)
            for s in stored:
                dve.sem_inc(s, 16)

            def take_x(q, p):
                dve.wait_ge(xt_ready, q + 1)
                dve.wait_ge(up_ready, q + 1)
                dve.tensor_copy(xT[:, p, :, :, :], X[:, p, :].rearrange("p (i k r) -> p i k r", i=2, k=KD)
                                ).then_inc(xt_done, 1)

            def product(q, p):
                dve.wait_ge(silu_done, q + 1)
                dve.wait_ge(tr_ready, q + 1)
                dve.tensor_tensor(h[:, p, :, :], g[:, p, :, :],
                                  U[:, p, :].rearrange("p (i f) -> p i f", i=2)[:, :, F:2 * F], ALU.mult
                                  ).then_inc(h_done, 1)

            def take_h(q, p):
                dve.wait_ge(tr_ready, q + 1 + CREDIT)
                dve.wait_ge(dn_ready, q + 1)
                dve.tensor_copy(hT[:, p, :, :], TT[:, p, 0:2 * P].rearrange("p (i r) -> p i r", i=2)
                                ).then_inc(ht_done, 1)

            def body(q, n, more=True):
                product(q, n % 2)
                if more:
                    take_x(q + 1, 1 - n % 2)
                take_h(q, n % 2)

            def first():
                take_x(0, 0)
                body(0, 0)

            pipelined(dve, first, body, lambda: body(N - 1, 1, more=False))

            flat = lambda m, i: m[:, J * i:J * i + J, :].rearrange("p t c -> p (t c)")
            for s in range(2):
                dve.wait_ge(sh_in[s], 16)
            for i in range(NT // J):
                tiles = range(J * i, J * i + J)
                ch.link(dve.tensor_tensor(flat(sh[:, 0, :, :], i), flat(sh[:, 0, :, :], i), flat(sh[:, 1, :, :], i), ALU.add))
                ch.link(dve.tensor_tensor(flat(sh[:, 0, :, :], i), flat(sh[:, 0, :, :], i), flat(G.x_sb, i), ALU.add))
                for t in tiles:
                    dve.wait_ge(gathered[t], 16 * K)
                for r in range(K):
                    for t in tiles:
                        ch.done(dve.scalar_tensor_tensor(sh[:, 0, t, :], ga[:, t, r, :], wgt[:, t, r:r + 1],
                                                         sh[:, 0, t, :], ALU.mult, ALU.add))
                    ch.wait()
                n = [ch.done(dve.bn_stats(st[:, j, :], sh[:, 0, t, :])) for j, t in enumerate(tiles)]
                for j in range(J):
                    ch.wait(n[j])
                    last_aggr = dve.bn_aggr(mv[:, j, :], st[:, j, :])
                last_aggr.then_inc(var_ready, 1)
                dve.wait_ge(rstd_ready, i + 1)
                for j, t in enumerate(tiles):
                    ch.done(dve.tensor_scalar(G.x_sb[:, t, :], sh[:, 0, t, :], mv[:, j, 0:1], rstd[:, j:j + 1],
                                              ALU.subtract, ALU.mult))
                ch.wait()

        @block.tensor
        def _(pe):
            def expert(u):
                return pe.value_load(ids[0:1, ds(u, 1)], min_val=0, max_val=EX - 1)

            def turn_x(q, n):
                pe.wait_ge(x_in[n], 16 * ((q - n) // NX) + 16)
                pe.wait_ge(xt_done, q + 1)
                for i in range(2):
                    for kk in range(KD):
                        mm = pe.transpose(X[:, n % 2, (KD * i + kk) * P:(KD * i + kk + 1) * P],
                                          xin[:, n, i, kk * P:(kk + 1) * P], G.ident_f[:, :])
                mm.then_inc(xt_ready, 1)

            def up(q, p):
                experts = [expert(2 * q + i) for i in range(2)]
                pe.wait_ge(xt_done, q + 1 + CREDIT)
                pe.wait_ge(h_done, q + 1)
                for i, e in enumerate(experts):
                    for kk in range(KD):
                        mm = pe.matmul(U[:, p, 2 * F * i:2 * F * (i + 1)], xT[:, p, i, kk, :],
                                       w13[:, ds(e, 1), kk, :].rearrange("p o f -> p (o f)"),
                                       start=(kk == 0), stop=(kk == KD - 1))
                mm.then_inc(up_ready, 1)

            def turn_h(q, p):
                pe.wait_ge(h_done, q + 1 + CREDIT)
                pe.wait_ge(ht_done, q + 1)
                for i in range(2):
                    mm = pe.transpose(TT[:, p, i * P:(i + 1) * P], h[:, p, i, :], G.ident_f[:, :])
                mm.then_inc(tr_ready, 1)

            def down(q, p):
                experts = [expert(2 * q + i) for i in range(2)]
                pe.wait_ge(ht_done, q + 1 + CREDIT)
                pe.wait_ge(y_done, q + 1)
                for i, e in enumerate(experts):
                    mm = pe.matmul(Y[:, p, i * D:(i + 1) * D], hT[:, p, i, :],
                                   w2[:, ds(e, 1), :].rearrange("p o c -> p (o c)"), start=True, stop=True)
                mm.then_inc(dn_ready, 1)

            def first():
                turn_x(0, 0)
                up(0, 0)
                turn_x(1, 1)
                turn_h(0, 0)

            def body(q, n):
                up(q, n % 2)
                turn_x(q + 1, (n + 1) % NX)
                down(q - 1, 1 - n % 2)
                turn_h(q, n % 2)

            def last():
                up(N - 1, 1)
                down(N - 2, 0)
                turn_h(N - 1, 1)
                down(N - 1, 1)

            pe.wait_ge(weights_in, 16 * WEIGHT_LOADS)
            pipelined(pe, first, body, last)
    sc.close()
    ws.close()


class Weights:

    up = down = None


class Globals:

    CONSTS = 1

    def __init__(self, nc, a, sc):
        self.nc, self.a = nc, a
        self.x_sb = sc.sb("x", [P, NT, D])
        self.ident_f = sc.sb("ident_f", [P, P])
        self.ident_b = sc.sb("ident_b", [P, P], BF16)
        self.x_loaded = sc.sem("x_loaded")
        self.const_ready = sc.sem("const_ready")
        self.const_step = sc.sem("const_step")
        self.passed = sc.sem("passed")
        self.x2_ready = sc.sem("x2_ready")
        self.zeroed = sc.sem("zeroed")
        self.up_in, self.down_in = sc.sem("up_in"), sc.sem("down_in")
        self.zero = sc.sb("zero", [P, D])
        self.W = None
        self.spent = []

    def causal_masks(self, sc):
        self.causal_q = sc.sb("causal_q", [P, 512])
        self.causal_k = sc.sb("causal_k", [P, P], BF16)

    def constants(self, pool):
        pool.memset(self.zero[:, :], 0.0)
        pool.memset(self.ident_f[:, :], 0.0)
        pool.memset(self.ident_b[:, :], 0.0)
        pool.memset(self.causal_q[:, :], 0.0)
        pool.memset(self.causal_k[:, :], 0.0).then_inc(self.const_step, 1)
        pool.wait_ge(self.const_step, 1)
        for ident in (self.ident_f, self.ident_b):
            pool.affine_select(out=ident[:, :], in_=ident[:, :], compare_op=ALU.not_equal, fill=1.0, base=0,
                               pattern=[[-1, P]], channel_multiplier=1)
        pool.affine_select(out=self.causal_q[:, 384:512], in_=self.causal_q[:, 384:512], compare_op=ALU.is_ge,
                           fill=NEG, base=0, pattern=[[-1, P]], channel_multiplier=1)
        pool.affine_select(out=self.causal_k[:, :], in_=self.causal_k[:, :], compare_op=ALU.is_ge,
                           fill=NEG, base=0, pattern=[[1, P]], channel_multiplier=-1).then_inc(self.const_ready, 1)

    UP_LOADS = DOWN_LOADS = 9 * 16

    def prefetch_up(self, sp):
        sp.wait_ge(self.const_ready, 1)
        for M, Xd in ((MIX0, self.a["Xd0"]), (MIX1, self.a["Xd1"])):
            rows_of = Xd[P * M.FIRST:P * (M.FIRST + M.ROUTED), :].rearrange("(n p) c -> p n c", p=P)
            sp.dma_start(rows_of, bcast(self.zero[:, :], 1, M.ROUTED)).then_inc(self.zeroed, 16)
        for e in range(9):
            sp.dma_start(self.W.up[:, e, :, :], self.a["up_w"][e]).then_inc(self.up_in, 16)

    def prefetch_down(self, sp):
        for e in range(9):
            sp.dma_start(self.W.down[:, e, :, :], self.a["down_w"][e]).then_inc(self.down_in, 16)


def store(nc, G, out):
    sc = Scope(nc, "st")
    stored = sc.sem("stored")
    with nc.Block() as block:
        @block.sync
        def _(sp):
            sp.dma_start(out.rearrange("(t p) c -> p t c", p=P), G.x_sb[:, :, :]).then_inc(stored, 16)
            sp.wait_ge(stored, 16)
    sc.close()


def build(nc, a, out):
    gs = Scope(nc, "g")
    G = Globals(nc, a, gs)
    a = dict(a)
    for M, n in ((MIX0, "0"), (MIX1, "1")):
        a["Xd" + n] = nc.dram_tensor("Xd" + n, (P * M.ITEMS, D), F32, kind="Internal").ap()
        a["Yd" + n] = nc.dram_tensor("Yd" + n, (P * M.ITEMS, D), F32, kind="Internal").ap()
    G.a = a
    wu, wd = Scope(nc, "wu"), Scope(nc, "wd")
    G.W = Weights()
    G.W.up = wu.sb("up", [P, 9, KD, 1024])
    ysc = Scope(nc, "ysc")
    y_sb = ysc.sb("y", [P, B * KVH, TB, REP * HD])
    attention_stage(nc, a, G, y_sb)
    xattn_stage(nc, a, G, y_sb)
    zero_semaphores(nc, G.spent)
    ysc.close()
    G.W.down = wd.sb("down", [P, 9, 8, D])
    moe0_stage(nc, a, G, G.W)
    wd.close()
    wu.close()
    rwkv_stage(nc, a, G)
    xattn1_stage(nc, a, G)
    zero_semaphores(nc, G.spent)
    moe1_stage(nc, a, G)
    store(nc, G, out)
    gs.close()


def rope_tables():
    half = HD // 2
    inv = (np.float32(1.0) / np.float32(10000.0) ** (np.arange(half, dtype=np.float32) / np.float32(half))).astype(np.float32)
    f = np.arange(S, dtype=np.float32)[:, None] * inv[None, :]
    cos = np.concatenate((np.cos(f), np.cos(f)), 1).astype(np.float32)
    sin = np.concatenate((-np.sin(f), np.sin(f)), 1).astype(np.float32)
    lay = lambda m: np.ascontiguousarray(m.reshape(TB, P, HD).transpose(1, 0, 2))
    return lay(cos), lay(sin)


def rows(w):
    return np.ascontiguousarray(w.reshape(-1, P, w.shape[-1]).transpose(1, 0, 2))


def layouts(inputs):
    i = {k: np.asarray(v) for k, v in inputs.items()}
    x = i["x"].reshape(T, D)
    m = {"x": rows(x), "xT": rows(np.ascontiguousarray(x.T)),
         "Wqkv": rows(np.concatenate([i["L0_attn_Wq"], i["L0_attn_Wk"], i["L0_attn_Wv"]], 1))}
    m["cos"], m["sin"] = rope_tables()
    m["Wo"] = rows(i["L0_attn_Wo"])
    m["WX"] = np.ascontiguousarray(np.stack([rows(i["L0_xattn_" + w]) for w in ("Wq", "Wk", "Wv", "Wo")], 1))
    ctx = i["ctx_1024"].reshape(-1, D)
    m["ctxT"] = rows(np.ascontiguousarray(ctx.T))
    for w in ("bq", "bk"):
        m[w] = np.ascontiguousarray(i["L0_xattn_" + w].reshape(KD, P).T)
    for w in ("bv", "bo"):
        m[w] = i["L0_xattn_" + w]
    m["gate0"], m["gate_b0"] = rows(i["L0_ffn_gate_w"]), i["L0_ffn_bias"]
    up = np.concatenate([i["L0_ffn_up_w"], i["L0_ffn_sw_up"][None]])
    m["up_w"] = np.ascontiguousarray(up.reshape(9, KD, P, 1024).transpose(0, 2, 1, 3))
    down = np.concatenate([i["L0_ffn_down_w"], i["L0_ffn_sw_down"][None]])
    m["down_w"] = np.ascontiguousarray(down.reshape(9, 8, P, D).transpose(0, 2, 1, 3))
    m["up_b"] = np.ascontiguousarray(np.concatenate([i["L0_ffn_up_b"], i["L0_ffn_sb_up"][None]])
                                     .reshape(9, 8, P).transpose(2, 0, 1))
    m["down_b"] = np.concatenate([i["L0_ffn_down_b"], i["L0_ffn_sb_down"][None]])
    m["mask0"], m["mask1"] = i["mask_BxS2_if1"], i["mask_BxS2_ik1"]
    m["rwkv_cols"] = np.ascontiguousarray(np.stack(
        [i["L1_attn_" + n].reshape(KD, P).T for n in
         ("ln_w", "ln_b", "time_mix_k", "time_mix_v", "time_mix_r", "time_decay", "time_first")], 1))
    m["rwkv_w"] = np.ascontiguousarray(np.stack([rows(i["L1_attn_" + n].T) for n in ("Wk", "Wv", "Wr", "Wo")], 1))
    m["ctx"] = np.ascontiguousarray(i["ctx_1024"].transpose(1, 0, 2))
    m["xq1"], m["xk1"] = rows(i["L1_xattn_Wq_w"]), rows(i["L1_xattn_Wk_w"].T)
    for w in ("q", "k"):
        m[f"b{w}1"] = np.ascontiguousarray(i[f"L1_xattn_W{w}_b"].reshape(KD, P).T)
    m["gate1"] = rows(i["L1_ffn_w_gate"].T)
    F = P
    both = np.concatenate([i["L1_ffn_w1_e"], i["L1_ffn_w1_s"].reshape(2, F, D)]), np.concatenate(
        [i["L1_ffn_w3_e"], i["L1_ffn_w3_s"].reshape(2, F, D)])
    w13 = np.concatenate(both, 1).transpose(2, 0, 1)
    m["w13"] = np.ascontiguousarray(w13.reshape(KD, P, -1, 2 * F).transpose(1, 2, 0, 3))
    w2s = i["L1_ffn_w2_s"].T.reshape(2, F, D)
    w2 = np.concatenate([i["L1_ffn_w2_e"].transpose(0, 2, 1), w2s])
    m["w2"] = np.ascontiguousarray(w2.transpose(1, 0, 2))
    return m


def kernel(**inputs):
    import concourse.bacc as bacc
    from concourse.bass_utils import run_bass_kernel_spmd

    nc = bacc.Bacc("TRN2", target_bir_lowering=False, num_devices=1)
    arrays = layouts(inputs)
    a = {n: nc.dram_tensor(n, m.shape, mybir.dt.from_np(m.dtype), kind="ExternalInput").ap() for n, m in arrays.items()}
    out = nc.dram_tensor("out", (T, D), F32, kind="ExternalOutput").ap()
    build(nc, a, out)
    result = run_bass_kernel_spmd(nc, [arrays], core_ids=[0])
    return result.results[0]["out"].reshape(B, S, D)
```
